# Optimizing a Trainium2 kernel written in Bass

```python
import numpy as np
import jax
import jax.numpy as jnp

def _softmax(x, axis=-1):
    return jax.nn.softmax(x, axis=axis)

def _gelu(x):
    return jax.nn.gelu(x, approximate=True)

def _silu(x):
    return jax.nn.silu(x)

def _sigmoid(x):
    return jax.nn.sigmoid(x)

def _layernorm(x, axis=-1, eps=1e-05):
    m = jnp.mean(x, axis=axis, keepdims=True)
    v = jnp.var(x, axis=axis, keepdims=True)
    return (x - m) / jnp.sqrt(v + eps)

def _scatter_add(tgt, idx, src, axis=0):
    return tgt.at[idx].add(src)

def _segment_sum(src, seg, n):
    return jax.ops.segment_sum(src, seg, n)
kernel_name = 'mk_adj_resnorm_d2_adj_r2_12f4eb'

def setup_inputs(seed: int=0):
    np.random.seed(seed)
    _w = jnp.asarray

    def _rec_inputs():
        import jax
        import jax.numpy as jnp
        _gk = jax.random.key(seed)
        x = -0.0002928 + 1 * jax.random.normal(jax.random.fold_in(_gk, 1), (16, 512, 256), jnp.float32)
        _w = (1.0 + jnp.arange(512, dtype=jnp.float32)) ** (-0.5)
        _w = _w / _w.mean()
        _pij = jnp.clip(0.0078125 * _w[:, None] * _w[None, :], 0.0, 1.0)
        _a = jax.random.uniform(jax.random.fold_in(_gk, 2), (16, 512, 512)) < _pij
        _a = jnp.logical_or(_a, jnp.eye(512, dtype=bool))
        _af = _a.astype(jnp.float32)
        _af = _af * jax.random.uniform(jax.random.fold_in(_gk, 3), (16, 512, 512), jnp.float32, 0.05, 1)
        adj = _af
        return (x, adj)
    x, adj = _rec_inputs()

    def _L0_gnn_setup():
        import jax, jax.numpy as jnp
        import numpy as np
        N = 4096
        F = 256
        C = 256
        key = jax.random.key(seed)
        k1, k2, k3 = jax.random.split(key, 3)
        X = jax.random.normal(k1, (1, N, F), dtype=jnp.float32)
        A = jax.random.uniform(k2, (1, N, N), dtype=jnp.float32)
        kernel = jax.random.normal(k3, (F, C), dtype=jnp.float32) * (1.0 / np.sqrt(F))
        bias = jnp.zeros((C,), dtype=jnp.float32)
        return {'X': X, 'A': A, 'kernel': kernel, 'bias': bias}
    _L0_gnn_all = _L0_gnn_setup()
    _L0_gnn_in = {k: v for k, v in _L0_gnn_all.items() if k in ('kernel', 'bias')}
    del _L0_gnn_all

    def _L1_gnn_setup():
        import jax, jax.numpy as jnp
        import numpy as np
        B, N, DIN, DOUT, K = (4, 1024, 256, 256, 3)
        key = jax.random.key(seed)
        ks = jax.random.split(key, 8)
        X = jax.random.normal(ks[0], (B, N, DIN), dtype=jnp.float32)
        A = jax.random.uniform(ks[1], (B, N, N), dtype=jnp.float32)
        Wv = jax.random.normal(ks[2], (DIN, DOUT), dtype=jnp.float32) * 0.02
        bv = jax.random.normal(ks[3], (DOUT,), dtype=jnp.float32) * 0.02
        aw = jax.random.normal(ks[4], (2 * DOUT, 1), dtype=jnp.float32) * 0.05
        ab = jax.random.normal(ks[5], (1,), dtype=jnp.float32) * 0.05
        Wk = jax.random.normal(ks[6], (K, DIN, DOUT), dtype=jnp.float32) * 0.02
        bk = jax.random.normal(ks[7], (K, DOUT), dtype=jnp.float32) * 0.02
        return {'X': X, 'A': A, 'Wv': Wv, 'bv': bv, 'aw': aw, 'ab': ab, 'Wk': Wk, 'bk': bk}
    _L1_gnn_all = _L1_gnn_setup()
    _L1_gnn_in = {k: v for k, v in _L1_gnn_all.items() if k in ('Wv', 'bv', 'aw', 'ab', 'Wk', 'bk')}
    del _L1_gnn_all
    return {'x': x, 'adj': adj, 'L0_gnn_kernel': _L0_gnn_in['kernel'], 'L0_gnn_bias': _L0_gnn_in['bias'], 'L1_gnn_Wv': _L1_gnn_in['Wv'], 'L1_gnn_bv': _L1_gnn_in['bv'], 'L1_gnn_aw': _L1_gnn_in['aw'], 'L1_gnn_ab': _L1_gnn_in['ab'], 'L1_gnn_Wk': _L1_gnn_in['Wk'], 'L1_gnn_bk': _L1_gnn_in['bk']}

def reference(x, adj, L0_gnn_kernel, L0_gnn_bias, L1_gnn_Wv, L1_gnn_bv, L1_gnn_aw, L1_gnn_ab, L1_gnn_Wk, L1_gnn_bk):
    import jax
    import jax.numpy as jnp

    def _L0_gnn_ref(X, A, kernel, bias):
        import jax, jax.numpy as jnp
        import numpy as np
        N = 4096
        F = 256
        C = 256
        Ah = A + jnp.eye(A.shape[-1], dtype=A.dtype)[None, :, :]
        dh = jax.lax.rsqrt(jnp.sum(Ah, axis=-1))
        An = dh[:, :, None] * Ah * dh[:, None, :]
        out = jnp.einsum('bnm,bmf,fc->bnc', An, X, kernel) + bias
        return jax.nn.relu(out)

    def _L1_gnn_ref(X, A, Wv, bv, aw, ab, Wk, bk):
        import jax, jax.numpy as jnp
        import numpy as np
        B, N, DIN, DOUT, K = (4, 1024, 256, 256, 3)
        d = Wv.shape[1]
        Xw = X @ Wv + bv
        sj = Xw @ aw[:d, 0]
        si = Xw @ aw[d:, 0]
        e = jax.nn.leaky_relu(sj[:, None, :] + si[:, :, None] + ab[0], negative_slope=0.2)
        alpha_matrix = A * jnp.exp(e)
        transition = alpha_matrix / (jnp.sum(alpha_matrix, axis=-1, keepdims=True) + 1e-12)
        H = jnp.zeros(X.shape[:-1] + (d,), dtype=X.dtype)
        Xk = X
        for k in range(Wk.shape[0]):
            H = H + Xk @ Wk[k] + bk[k]
            Xk = jnp.einsum('bij,bjd->bid', transition, Xk)
        return jax.nn.relu(H)
    x = _layernorm(x + _L0_gnn_ref(x, adj, L0_gnn_kernel, L0_gnn_bias), axis=-1)
    x = _layernorm(x + _L1_gnn_ref(x, adj, L1_gnn_Wv, L1_gnn_bv, L1_gnn_aw, L1_gnn_ab, L1_gnn_Wk, L1_gnn_bk), axis=-1)
    return x

_drawn_inputs = setup_inputs


def setup_inputs(seed=0):
    import zlib

    import numpy as np

    out = dict(_drawn_inputs(seed))
    spreads = {'L0_gnn_bias': (0.0, 0.1)}
    factors = {'L1_gnn_Wv': 2.96, 'L1_gnn_bv': 8.0, 'L1_gnn_aw': 3.019}
    for name, (base, spread) in spreads.items():
        noise = np.random.default_rng([zlib.crc32(name.encode()), seed]).standard_normal(out[name].shape)
        drawn = base * np.exp(spread * noise) if base else spread * noise
        out[name] = jnp.asarray(drawn.astype(out[name].dtype))
    for name, factor in factors.items():
        out[name] = (out[name] * factor).astype(out[name].dtype)
    return out
```

```python
from contextlib import ExitStack

import concourse.bass as bass
from concourse import mybir

F32 = mybir.dt.float32
F32R = mybir.dt.float32r
ALU = mybir.AluOpType
ACT = mybir.ActivationFunctionType
AX_X = mybir.AxisListType.X

P = 128
SLOPE = 0.2
NORM_EPS = 1e-5
SUM_EPS = 1e-12


def graph_layers(nc, x, adj, adj_t, kern, bias, wv, bv, aw, ab, wk, bk, out):
    G, N, F = x.shape
    NB = N // P
    FB = F // P
    FS = NB // FB
    NE = F + 2
    S_J, S_I = F, F + 1
    assert NB == 4 and FB == 2 and G % 2 == 0

    x_rows = x.rearrange("g (b p) f -> (g b) p f", p=P)
    adj_rows = adj.rearrange("g (b p) m -> (g b) p m", p=P)
    adj_t_rows = adj_t.rearrange("g (b p) m -> (g b) p m", p=P)
    out_rows = out.rearrange("g (b p) f -> (g b) p f", p=P)

    def graph_of(rows, t):
        return rows[bass.ds(t, NB), :, :].rearrange("b p f -> p b f")

    with ExitStack() as ctx:
        def sb(name, shape, dt=F32):
            return ctx.enter_context(nc.sbuf_tensor(name, shape, dt))

        def sem(name):
            return ctx.enter_context(nc.semaphore(name))

        agg_ps = [ctx.enter_context(nc.psum_tensor(f"agg_ps{f}", [P, N], F32)) for f in range(FB)]
        ring = [ctx.enter_context(nc.psum_tensor(f"ring{i}", [P, 512], F32)) for i in range(NB)]
        turn_ps = [ctx.enter_context(nc.psum_tensor(f"turn_ps{f}", [P, N], F32)) for f in range(FB)]
        target_ps = turn_ps[0]

        w2s_hi, w2s_lo = sb("w2s_hi", [P, FB, NE], F32R), sb("w2s_lo", [P, FB, NE], F32R)
        w10_hi, w10_lo = sb("w10_hi", [P, FB, 2 * F], F32R), sb("w10_lo", [P, FB, 2 * F], F32R)
        kern_hi, kern_lo = sb("kern_hi", [P, FB, F], F32R), sb("kern_lo", [P, FB, F], F32R)
        bias0 = sb("bias0", [P, F])
        bias1 = sb("bias1", [P, F])
        score_bias = sb("score_bias", [P, 1])
        ident = sb("ident", [P, P])
        ones4 = sb("ones4", [P, NB])
        minus_half = sb("minus_half", [P, NB])

        a_t = [sb(f"a_t{k}", [P, NB, N]) for k in range(2)]
        a_nat = sb("a_nat", [P, NB, N])
        xin = [sb(f"xin{k}", [P, NB, F]) for k in range(2)]
        ah_hi, ah_lo = sb("ah_hi", [P, NB, N], F32R), sb("ah_lo", [P, NB, N], F32R)
        diag = sb("diag", [P, NB, P])
        deg = sb("deg", [P, NB])
        deg1 = sb("deg1", [P, NB])
        dh = [sb(f"dh{k}", [P, NB]) for k in range(2)]
        xd_hi, xd_lo = sb("xd_hi", [P, NB, F], F32R), sb("xd_lo", [P, NB, F], F32R)
        y_hi, y_lo = sb("y_hi", [P, FB, N], F32R), sb("y_lo", [P, FB, N], F32R)
        h0 = sb("h0", [P, NB, F])
        r0 = sb("r0", [P, NB, F])
        x1 = [sb(f"x1_{k}", [P, NB, F]) for k in range(2)]
        x1t_hi, x1t_lo = sb("x1t_hi", [P, FB, N], F32R), sb("x1t_lo", [P, FB, N], F32R)
        score = sb("score", [P, NB, 2])
        sj = sb("sj", [P, NB])
        sj_slope = sb("sj_slope", [P, NB])
        u0 = sb("u0", [P, NB, F])
        u1 = sb("u1", [P, NB, F])
        v2_hi, v2_lo = sb("v2_hi", [P, NB, NE], F32R), sb("v2_lo", [P, NB, F], F32R)
        exp_a = sb("exp_a", [P, NB, N])
        exp_b = sb("exp_b", [P, NB, N])
        s_hi, s_lo = sb("s_hi", [P, NB, N], F32R), sb("s_lo", [P, NB, N], F32R)
        row_sum = sb("row_sum", [P, NB])
        row_inv = sb("row_inv", [P, NB])
        v1 = sb("v1", [P, NB, F])
        v1_hi, v1_lo = sb("v1_hi", [P, NB, F], F32R), sb("v1_lo", [P, NB, F], F32R)
        h1 = sb("h1", [P, NB, F])
        r1 = sb("r1", [P, NB, F])
        y_out = sb("y_out", [P, NB, F])
        shift1 = sb("shift1", [P, NB])
        stats = [sb(f"stats{k}", [P, NB, 6]) for k in range(2)]
        mean_var = [sb(f"mean_var{k}", [P, NB, 2]) for k in range(2)]
        var_eps = [sb(f"var_eps{k}", [P, NB]) for k in range(2)]
        rstd = [sb(f"rstd{k}", [P, NB]) for k in range(2)]
        pace = sb("pace", [P, 1])

        w2s_raw = exp_a[:, 0:2, :].rearrange("p b n -> p (b n)")[:, 0:FB * NE].rearrange("p (f n) -> p f n", f=FB)
        w10_raw = exp_b[:, 0:2, :]
        wv_raw = exp_a[:, 2, :].rearrange("p (f n) -> p f n", f=FB)
        kern_raw = exp_a[:, 3, :].rearrange("p (f n) -> p f n", f=FB)
        aw_rep = exp_b[:, 2, :].rearrange("p (k n) -> p k n", k=2)
        bv_rep = exp_b[:, 3, 0:F]
        dots = exp_b[:, 3, F:2 * F]
        bk_rep = h1[:, 0:3, :]
        ab_rep = sb("ab_rep", [P, 1])
        bv_dot = sb("bv_dot", [P, 2])

        ld_w = sem("ld_w")
        ld_at = [sem(f"ld_at{k}") for k in range(2)]
        ld_x = [sem(f"ld_x{k}") for k in range(2)]
        ld_nat = sem("ld_nat")
        out_free = sem("out_free")
        const_ready = sem("const_ready")
        set_dve = sem("set_dve")
        weights_ready = sem("weights_ready")
        agg_done = sem("agg_done")
        kern_done = sem("kern_done")
        turn_done = sem("turn_done")
        u2_done = sem("u2_done")
        u10_done = sem("u10_done")
        target_done = sem("target_done")
        sv2_done = sem("sv2_done")
        sv1_done = sem("sv1_done")
        ah_hi_done = sem("ah_hi_done")
        xd_hi_done = sem("xd_hi_done")
        y_hi_done = sem("y_hi_done")
        x1t_hi_done = sem("x1t_hi_done")
        v2_hi_done = sem("v2_hi_done")
        u1_done = sem("u1_done")
        exp_done = sem("exp_done")
        s_hi_done = sem("s_hi_done")
        v1_hi_done = sem("v1_hi_done")
        out_done = sem("out_done")
        xd_lo_done = sem("xd_lo_done")
        y_lo_done = sem("y_lo_done")
        h0_done = sem("h0_done")
        r0_done = sem("r0_done")
        stat0_done = sem("stat0_done")
        agr0_done = sem("agr0_done")
        eps0_done = sem("eps0_done")
        x1_done = sem("x1_done")
        x1t_lo_done = sem("x1t_lo_done")
        score_done = sem("score_done")
        sj_done = sem("sj_done")
        v2_lo_done = sem("v2_lo_done")
        u0_done = sem("u0_done")
        s_done = sem("s_done")
        s_lo_done = sem("s_lo_done")
        sum_done = sem("sum_done")
        inv_done = sem("inv_done")
        v1_done = sem("v1_done")
        v1_lo_done = sem("v1_lo_done")
        h1_done = sem("h1_done")
        r1_done = sem("r1_done")
        stat1_done = sem("stat1_done")
        agr1_done = sem("agr1_done")
        eps1_done = sem("eps1_done")
        shift1_done = sem("shift1_done")
        deg_done = sem("deg_done")
        deg1_done = sem("deg1_done")
        dh_done = sem("dh_done")
        diag_done = sem("diag_done")
        ah_lo_done = sem("ah_lo_done")
        max_done = sem("max_done")
        rstd0_done = sem("rstd0_done")
        rstd1_done = sem("rstd1_done")

        def loaded(k, t):
            return t * 2 + (16 if k == 0 else 8)

        def diagonal(tensor, width):
            full = tensor[:, 0, 0:P]
            return bass.AP(full.tensor, full.offset, [list(full.ap[0]), [width + P, NB], [1, P]])

        block = ctx.enter_context(nc.Block())

        @block.sync
        def _(sp):
            def load_x(t, k):
                sp.dma_start(xin[k][:, :, :], graph_of(x_rows, t)).then_inc(ld_x[k], 16)

            def load_nat(t):
                sp.dma_start(a_nat[:, :, :], graph_of(adj_rows, t)).then_inc(ld_nat, 16)

            def load_at(t, k):
                sp.dma_start(a_t[k][:, :, :], graph_of(adj_t_rows, t)).then_inc(ld_at[k], 16)

            def store(t):
                sp.wait_ge(out_done, t + 4)
                sp.dma_start(graph_of(out_rows, t), y_out[:, :, :]).then_inc(out_free, 16)

            def ahead(t, k):
                sp.wait_ge(x1_done, t + 4)
                load_x(t + 8, k)
                sp.wait_ge(deg_done, t + 8)
                load_nat(t + 8)
                sp.wait_ge(s_done, t + 4)
                load_at(t + 8, k)

            load_nat(0)
            load_at(0, 0)
            load_x(0, 0)
            sp.wait_ge(deg_done, 4)
            load_nat(4)
            load_x(4, 1)
            load_at(4, 1)
            ahead(0, 0)
            with sp.Fori(4, 4 * (G - 4) - 3, 8) as t0:
                for half in range(2):
                    t = t0 + 4 * half
                    ahead(t, 1 - half)
                    store(t - 4)
            ahead(4 * (G - 3), 1)
            for g in range(G - 4, G):
                store(4 * g)
            sp.wait_ge(out_free, 16 * (G + 1))

        @block.tensor
        def _(pe):
            def three_passes(dst, terms, width=None):
                for n, (l_hi, l_lo, r_hi, r_lo) in enumerate(terms):
                    pe.matmul(dst[:, 0:r_hi.shape[-1]], l_hi, r_hi, start=(n == 0), stop=False)
                    pe.matmul(dst[:, 0:r_lo.shape[-1]], l_hi, r_lo, start=False, stop=False)
                    last = pe.matmul(dst[:, 0:r_hi.shape[-1]], l_lo, r_hi, start=False,
                                     stop=(n == len(terms) - 1))
                return last

            def aggregate(t, first=False):
                pe.wait_ge(ah_lo_done, t + 4)
                pe.wait_ge(xd_lo_done, t + 4)
                for f in range(FB):
                    if not first:
                        pe.wait_ge(y_lo_done, t - 4 + FS * (f + 1))
                    cols = slice(f * P, (f + 1) * P)
                    three_passes(agg_ps[f], [(xd_hi[:, j, cols], xd_lo[:, j, cols], ah_hi[:, j, :], ah_lo[:, j, :])
                                             for j in range(NB)]).then_inc(agg_done, FS)

            def times_kernel(t, first=False):
                pe.wait_ge(y_lo_done, t + 4)
                for i in range(NB):
                    if not first:
                        pe.wait_ge(v1_done, t - 4 + i + 1)
                    rows = slice(i * P, (i + 1) * P)
                    three_passes(ring[i], [(y_hi[:, f, rows], y_lo[:, f, rows], kern_hi[:, f, :], kern_lo[:, f, :])
                                           for f in range(FB)]).then_inc(kern_done, 1)

            def turn_x1(t, k, first=False):
                pe.wait_ge(x1_done, t + 4)
                for f in range(FB):
                    if not first:
                        pe.wait_ge(exp_done if f == 0 else x1t_lo_done, t)
                    for i in range(NB):
                        last = pe.transpose(turn_ps[f][:, i * P:(i + 1) * P], x1[k][:, i, f * P:(f + 1) * P],
                                            ident[:, :])
                    last.then_inc(turn_done, FS)

            def x1_rows(f, i):
                rows = slice(i * P, (i + 1) * P)
                return x1t_hi[:, f, rows], x1t_lo[:, f, rows]

            def times_w2(t, first=False):
                pe.wait_ge(x1t_lo_done, t + 4)
                for i in range(NB):
                    pe.wait_ge(h0_done if first else h1_done, (t + 4 if first else t) - 4 + i + 1)
                    three_passes(ring[i], [(*x1_rows(f, i), w2s_hi[:, f, :], w2s_lo[:, f, :]) for f in range(FB)])\
                        .then_inc(u2_done, 1)

            def times_w10(t, i):
                pe.wait_ge(v2_lo_done, t + i + 1)
                three_passes(ring[i], [(*x1_rows(f, i), w10_hi[:, f, :], w10_lo[:, f, :]) for f in range(FB)])\
                    .then_inc(u10_done, 1)

            def spread_targets(t):
                pe.wait_ge(score_done, t + 4)
                for i in range(NB):
                    last = pe.transpose(target_ps[:, i * P:(i + 1) * P],
                                        score[:, i, 1:2].to_broadcast([P, P]), ident[:, :])
                last.then_inc(target_done, 4)

            def times_s_v2(t):
                pe.wait_ge(s_lo_done, t + 4)
                for i in range(NB):
                    pe.wait_ge(u1_done, t + i + 1)
                    pe.wait_ge(u0_done, t + i + 1)
                    rows = slice(i * P, (i + 1) * P)
                    three_passes(ring[i], [(s_hi[:, j, rows], s_lo[:, j, rows], v2_hi[:, j, :], v2_lo[:, j, :])
                                           for j in range(NB)]).then_inc(sv2_done, 1)

            def times_s_v1(t, i, last=False):
                if i == 0:
                    pe.wait_ge(v1_lo_done, t + 4)
                if not last:
                    pe.wait_ge(h0_done, t + 4 + i + 1)
                rows = slice(i * P, (i + 1) * P)
                three_passes(ring[i], [(s_hi[:, j, rows], s_lo[:, j, rows], v1_hi[:, j, :], v1_lo[:, j, :])
                                       for j in range(NB)]).then_inc(sv1_done, 1)

            def graph(t, k, first=False, last=False):
                times_w2(t, first)
                times_w10(t, 0)
                spread_targets(t)
                for i in range(1, NB):
                    times_w10(t, i)
                if not last:
                    aggregate(t + 4)
                times_s_v2(t)
                if not last:
                    times_kernel(t + 4)
                for i in range(NB):
                    times_s_v1(t, i, last)
                    if i == 2 and not last:
                        turn_x1(t + 4, 1 - k)

            pe.wait_ge(const_ready, 4)
            pe.wait_ge(weights_ready, 1)
            aggregate(0, first=True)
            times_kernel(0, first=True)
            turn_x1(0, 0, first=True)
            graph(0, 0, first=True)
            with pe.Fori(4, 4 * (G - 2) - 3, 8) as t0:
                for half in range(2):
                    graph(t0 + 4 * half, 1 - half)
            graph(4 * (G - 1), 1, last=True)

        @block.scalar
        def _(act):
            def high_adj(t, k, first=False):
                act.wait_ge(ld_at[k], loaded(k, t))
                if not first:
                    act.wait_ge(agg_done, t)
                act.activation(ah_hi[:, :, :], a_t[k][:, :, :], ACT.Copy).then_inc(ah_hi_done, 4)

            def row_sums(t):
                act.wait_ge(ld_nat, t * 4 + 16)
                for i in range(NB):
                    act.activation(a_nat[:, i, :], a_nat[:, i, :], ACT.Copy, accum_out=deg[:, i:i + 1])\
                       .then_inc(deg_done, 1)

            def high_xd(t, k, first=False):
                act.wait_ge(ld_x[k], loaded(k, t))
                act.wait_ge(dh_done, t + 4)
                if not first:
                    act.wait_ge(agg_done, t)
                for i in range(NB):
                    act.activation(xd_hi[:, i, :], xin[k][:, i, :], ACT.Copy, scale=dh[k][:, i:i + 1])\
                       .then_inc(xd_hi_done, 1)

            def high_y(t):
                for f in range(FB):
                    act.wait_ge(agg_done, t + FS * (f + 1))
                    act.activation(y_hi[:, f, :], agg_ps[f][:, :], ACT.Copy).then_inc(y_hi_done, FS)

            def high_x1t(t):
                for f in range(FB):
                    act.wait_ge(turn_done, t + FS * (f + 1))
                    act.activation(x1t_hi[:, f, :], turn_ps[f][:, :], ACT.Copy).then_inc(x1t_hi_done, FS)

            def high_v2(t):
                for i in range(NB):
                    act.wait_ge(score_done, t + i + 1)
                    act.activation(v2_hi[:, i, 0:F], ring[i][:, 0:F], ACT.Copy).then_inc(v2_hi_done, 1)

            def take_u1(t, i):
                act.wait_ge(u10_done, t + i + 1)
                act.activation(u1[:, i, :], ring[i][:, 0:F], ACT.Copy).then_inc(u1_done, 1)

            def exps(t, j):
                if j == 0:
                    act.wait_ge(target_done, t + 4)
                    act.wait_ge(sj_done, t + 4)
                act.activation(exp_a[:, j, :], target_ps[:, :], ACT.Exp, bias=sj[:, j:j + 1])
                act.activation(exp_b[:, j, :], target_ps[:, :], ACT.Exp, bias=sj_slope[:, j:j + 1], scale=SLOPE)\
                   .then_inc(exp_done, 1)

            def high_s(t, j):
                act.wait_ge(s_done, t + j + 1)
                act.activation(s_hi[:, j, :], exp_b[:, j, :], ACT.Copy).then_inc(s_hi_done, 1)

            def high_v1(t):
                for i in range(0, NB, 2):
                    act.wait_ge(v1_done, t + i + 2)
                    act.activation(v1_hi[:, i:i + 2, :], v1[:, i:i + 2, :], ACT.Copy).then_inc(v1_hi_done, 2)

            def norm_out(t):
                act.wait_ge(shift1_done, t + 4)
                act.wait_ge(out_free, t * 4 + 16)
                for i in range(NB):
                    act.activation(y_out[:, i, :], r1[:, i, :], ACT.Identity, scale=rstd[1][:, i:i + 1],
                                   bias=shift1[:, i:i + 1]).then_inc(out_done, 1)

            def graph(t, k, first=False, last=False, ahead=True):
                high_v2(t)
                if not last:
                    high_xd(t + 4, 1 - k)
                take_u1(t, 0)
                exps(t, 0)
                take_u1(t, 1)
                exps(t, 1)
                take_u1(t, 2)
                exps(t, 2)
                take_u1(t, 3)
                high_s(t, 0)
                exps(t, 3)
                for j in range(1, NB):
                    high_s(t, j)
                if not last:
                    high_y(t + 4)
                if not first:
                    norm_out(t - 4)
                high_v1(t)
                if ahead:
                    row_sums(t + 8)
                    high_adj(t + 8, k)
                if not last:
                    high_x1t(t + 4)

            row_sums(0)
            high_adj(0, 0, first=True)
            high_xd(0, 0, first=True)
            row_sums(4)
            high_y(0)
            high_adj(4, 1)
            high_x1t(0)
            graph(0, 0, first=True)
            with act.Fori(4, 4 * (G - 4) - 3, 8) as t0:
                for half in range(2):
                    graph(t0 + 4 * half, 1 - half)
            graph(4 * (G - 3), 1)
            graph(4 * (G - 2), 0, ahead=False)
            graph(4 * (G - 1), 1, last=True, ahead=False)
            norm_out(4 * (G - 1))

        @block.vector
        def _(dve):
            def low_xd(t, k):
                for i in range(NB):
                    dve.wait_ge(xd_hi_done, t + i + 1)
                    dve.scalar_tensor_tensor(xd_lo[:, i, :], xin[k][:, i, :], dh[k][:, i:i + 1],
                                             xd_hi[:, i, :].bitcast(F32), ALU.mult, ALU.subtract)\
                       .then_inc(xd_lo_done, 1)

            def low_y(t):
                for f in range(FB):
                    dve.wait_ge(y_hi_done, t + FS * (f + 1))
                    dve.tensor_tensor(y_lo[:, f, :], agg_ps[f][:, :], y_hi[:, f, :].bitcast(F32), ALU.subtract)\
                       .then_inc(y_lo_done, FS)

            def layer0_out(t, k):
                for s in range(NB + 2):
                    if s < NB:
                        dve.wait_ge(kern_done, t + s + 1)
                        dve.scalar_tensor_tensor(h0[:, s, :], ring[s][:, 0:F], dh[k][:, s:s + 1], bias0[:, :],
                                                 ALU.mult, ALU.add).then_inc(h0_done, 1)
                    if 1 <= s <= NB:
                        i = s - 1
                        dve.wait_ge(h0_done, t + i + 1)
                        dve.scalar_tensor_tensor(r0[:, i, :], h0[:, i, :], 0.0, xin[k][:, i, :],
                                                 ALU.max, ALU.add).then_inc(r0_done, 1)
                    if s >= 2:
                        i = s - 2
                        dve.wait_ge(r0_done, t + i + 1)
                        dve.bn_stats(stats[0][:, i, :], r0[:, i, :]).then_inc(stat0_done, 1)

            def moments(t, layer, stat_done, agr_done, eps_done):
                dve.wait_ge(stat_done, t + 4)
                dve.memset(pace[:, :], 0.0)
                for i in range(NB):
                    dve.bn_aggr(mean_var[layer][:, i, :], stats[layer][:, i, :]).then_inc(agr_done, 1)
                dve.wait_ge(agr_done, t + 4)
                dve.tensor_scalar(var_eps[layer][:, :], mean_var[layer][:, :, 1], NORM_EPS, None, ALU.add)\
                   .then_inc(eps_done, 4)

            def norm_x1(t, k):
                dve.wait_ge(rstd0_done, t + 4)
                for i in range(NB):
                    dve.tensor_scalar(x1[k][:, i, :], r0[:, i, :], mean_var[0][:, i, 0:1], rstd[0][:, i:i + 1],
                                      ALU.subtract, ALU.mult).then_inc(x1_done, 1)

            def low_x1t(t):
                for f in range(FB):
                    dve.wait_ge(x1t_hi_done, t + FS * (f + 1))
                    dve.tensor_tensor(x1t_lo[:, f, :], turn_ps[f][:, :], x1t_hi[:, f, :].bitcast(F32), ALU.subtract)\
                       .then_inc(x1t_lo_done, FS)

            def take_v2(t):
                for s in range(NB + 1):
                    if s < NB:
                        dve.wait_ge(u2_done, t + s + 1)
                        dve.tensor_copy(score[:, s, :], ring[s][:, S_J:S_I + 1]).then_inc(score_done, 1)
                    if s >= 1:
                        i = s - 1
                        dve.wait_ge(v2_hi_done, t + i + 1)
                        dve.tensor_tensor(v2_lo[:, i, :], ring[i][:, 0:F], v2_hi[:, i, 0:F].bitcast(F32),
                                          ALU.subtract).then_inc(v2_lo_done, 1)

            def source_scores(t):
                dve.wait_ge(score_done, t + 4)
                dve.tensor_scalar(sj[:, :], score[:, :, 0], score_bias[:, 0:1], None, ALU.add).then_inc(sj_done, 2)
                dve.tensor_scalar(sj_slope[:, :], score[:, :, 0], score_bias[:, 0:1], SLOPE, ALU.add, ALU.mult)\
                   .then_inc(sj_done, 2)

            def take_u0(t, i):
                dve.wait_ge(u1_done, t + i + 1)
                dve.tensor_tensor(u0[:, i, :], ring[i][:, F:2 * F], bias1[:, :], ALU.add).then_inc(u0_done, 1)

            def larger_exp(t, j):
                dve.wait_ge(exp_done, t + j + 1)
                dve.tensor_tensor(exp_a[:, j, :], exp_a[:, j, :], exp_b[:, j, :], ALU.max).then_inc(max_done, 1)

            def low_s(t, j):
                dve.wait_ge(s_hi_done, t + j + 1)
                dve.tensor_tensor(s_lo[:, j, :], exp_b[:, j, :], s_hi[:, j, :].bitcast(F32), ALU.subtract)\
                   .then_inc(s_lo_done, 1)

            def make_v1(t):
                for i in range(NB):
                    dve.wait_ge(sv2_done, t + i + 1)
                    dve.tensor_scalar(row_sum[:, i:i + 1], ring[i][:, F:F + 1], SUM_EPS, None, ALU.add)\
                       .then_inc(sum_done, 1)
                    dve.wait_ge(sum_done, t + i + 1)
                    dve.reciprocal(row_inv[:, i:i + 1], row_sum[:, i:i + 1]).then_inc(inv_done, 1)
                    dve.wait_ge(inv_done, t + i + 1)
                    dve.scalar_tensor_tensor(v1[:, i, :], ring[i][:, 0:F], row_inv[:, i:i + 1], u1[:, i, :],
                                             ALU.mult, ALU.add).then_inc(v1_done, 1)

            def low_v1(t):
                for i in range(0, NB, 2):
                    dve.wait_ge(v1_hi_done, t + i + 2)
                    dve.tensor_tensor(v1_lo[:, i:i + 2, :], v1[:, i:i + 2, :], v1_hi[:, i:i + 2, :].bitcast(F32),
                                      ALU.subtract).then_inc(v1_lo_done, 2)

            def make_h1(t, i):
                dve.wait_ge(sv1_done, t + i + 1)
                dve.scalar_tensor_tensor(h1[:, i, :], ring[i][:, 0:F], row_inv[:, i:i + 1], u0[:, i, :],
                                         ALU.mult, ALU.add).then_inc(h1_done, 1)

            def layer1_out(t, k):
                dve.wait_ge(h1_done, t + 4)
                dve.scalar_tensor_tensor(r1[:, :, :], h1[:, :, :], 0.0, x1[k][:, :, :], ALU.max, ALU.add)\
                   .then_inc(r1_done, 4)
                dve.wait_ge(r1_done, t + 4)
                for i in range(NB):
                    dve.bn_stats(stats[1][:, i, :], r1[:, i, :]).then_inc(stat1_done, 1)
                moments(t, 1, stat1_done, agr1_done, eps1_done)

            def shift_out(t):
                dve.wait_ge(rstd1_done, t + 4)
                dve.scalar_tensor_tensor(shift1[:, :], mean_var[1][:, :, 0], -1.0, rstd[1][:, :],
                                         ALU.mult, ALU.mult).then_inc(shift1_done, 4)

            def graph(t, k, first=False, last=False):
                take_v2(t)
                source_scores(t)
                if not last:
                    low_xd(t + 4, 1 - k)
                take_u0(t, 0)
                if not first:
                    layer1_out(t - 4, 1 - k)
                for i in range(1, NB):
                    take_u0(t, i)
                    larger_exp(t, i - 1)
                if not first:
                    shift_out(t - 4)
                low_s(t, 0)
                larger_exp(t, NB - 1)
                for j in range(1, NB):
                    low_s(t, j)
                if not last:
                    low_y(t + 4)
                make_v1(t)
                low_v1(t)
                if not last:
                    layer0_out(t + 4, 1 - k)
                    moments(t + 4, 0, stat0_done, agr0_done, eps0_done)
                    make_h1(t, 0)
                    norm_x1(t + 4, 1 - k)
                    make_h1(t, 1)
                    make_h1(t, 2)
                    low_x1t(t + 4)
                    make_h1(t, 3)
                else:
                    for i in range(NB):
                        make_h1(t, i)

            dve.memset(v2_hi[:, :, F:F + 1].bitcast(F32), 1.0)
            dve.memset(v2_hi[:, :, F + 1:F + 2].bitcast(F32), 0.0)
            dve.wait_ge(ld_w, 16 * 11)
            done = 0
            for c in range(2):
                for f in range(FB):
                    dve.tensor_tensor_reduce(dots, wv_raw[:, f, :], aw_rep[:, c, :], 1.0, 0.0, ALU.mult, ALU.add,
                                             w2s_raw[:, f, F + c:F + c + 1]).then_inc(set_dve, 1)
                    done += 1
                    dve.wait_ge(set_dve, done)
                dve.tensor_tensor_reduce(dots, bv_rep, aw_rep[:, c, :], 1.0, 0.0, ALU.mult, ALU.add,
                                         bv_dot[:, c:c + 1]).then_inc(set_dve, 1)
                done += 1
                dve.wait_ge(set_dve, done)
            dve.scalar_tensor_tensor(score_bias[:, :], bv_dot[:, 0:1], ab_rep[:, :], bv_dot[:, 1:2],
                                     ALU.add, ALU.add)
            dve.tensor_tensor(bias1[:, :], bk_rep[:, 0, :], bk_rep[:, 1, :], ALU.add)
            for hi, raw in ((w2s_hi, w2s_raw), (w10_hi, w10_raw), (kern_hi, kern_raw)):
                last = dve.tensor_copy(hi[:, :, :], raw)
            last.then_inc(set_dve, 1)
            done += 1
            dve.wait_ge(set_dve, done)
            dve.tensor_tensor(bias1[:, :], bias1[:, :], bk_rep[:, 2, :], ALU.add)
            for lo, raw, hi in ((w2s_lo, w2s_raw, w2s_hi), (w10_lo, w10_raw, w10_hi), (kern_lo, kern_raw, kern_hi)):
                last = dve.tensor_tensor(lo[:, :, :], raw, hi[:, :, :].bitcast(F32), ALU.subtract)
            last.then_inc(weights_ready, 1)
            dve.wait_ge(weights_ready, 1)

            low_xd(0, 0)
            low_y(0)
            layer0_out(0, 0)
            moments(0, 0, stat0_done, agr0_done, eps0_done)
            norm_x1(0, 0)
            low_x1t(0)
            graph(0, 0, first=True)
            with dve.Fori(4, 4 * (G - 2) - 3, 8) as t0:
                for half in range(2):
                    graph(t0 + 4 * half, 1 - half)
            graph(4 * (G - 1), 1, last=True)
            layer1_out(4 * (G - 1), 1)
            shift_out(4 * (G - 1))

        @block.gpsimd
        def _(pool):
            def make_s(t, k, j):
                if j == 0:
                    pool.wait_ge(ld_at[k], loaded(k, t))
                pool.wait_ge(max_done, t + j + 1)
                pool.tensor_tensor(exp_b[:, j, :], a_t[k][:, j, :], exp_a[:, j, :], ALU.mult).then_inc(s_done, 1)

            def degrees(t, k):
                pool.wait_ge(deg_done, t + 4)
                pool.tensor_tensor(deg1[:, :], deg[:, :], ones4[:, :], ALU.add).then_inc(deg1_done, 4)
                pool.wait_ge(deg1_done, t + 4)
                pool.tensor_tensor(dh[k][:, :], deg1[:, :], minus_half[:, :], ALU.pow).then_inc(dh_done, 4)

            def low_adj(t, k):
                pool.wait_ge(ah_hi_done, t + 4)
                on_diagonal = ident[:, :].unsqueeze(1).to_broadcast([P, NB, P])
                pool.tensor_tensor(diagonal(ah_hi, N), diagonal(a_t[k], N), on_diagonal, ALU.add)\
                    .then_inc(diag_done, 2)
                pool.tensor_tensor(diag[:, :, :], diagonal(a_t[k], N), on_diagonal, ALU.add).then_inc(diag_done, 2)
                pool.wait_ge(diag_done, t + 4)
                pool.tensor_tensor(ah_lo[:, :, :], a_t[k][:, :, :], ah_hi[:, :, :].bitcast(F32), ALU.subtract)\
                    .then_inc(ah_lo_done, 2)
                pool.wait_ge(ah_lo_done, t + 2)
                pool.tensor_tensor(diagonal(ah_lo, N), diag[:, :, :], diagonal(ah_hi, N).bitcast(F32), ALU.subtract)\
                    .then_inc(ah_lo_done, 2)

            def root(t, layer, eps_done, rstd_done):
                pool.wait_ge(eps_done, t + 4)
                pool.tensor_tensor(rstd[layer][:, :], var_eps[layer][:, :], minus_half[:, :], ALU.pow)\
                    .then_inc(rstd_done, 4)

            def graph(t, k, first=False, last=False, ahead=True):
                if not first:
                    root(t - 4, 1, eps1_done, rstd1_done)
                for j in range(NB):
                    make_s(t, k, j)
                if ahead:
                    degrees(t + 8, k)
                if not last:
                    root(t + 4, 0, eps0_done, rstd0_done)
                if ahead:
                    low_adj(t + 8, k)

            pool.memset(ident[:, :], 0.0).then_inc(const_ready, 1)
            pool.memset(ones4[:, :], 1.0).then_inc(const_ready, 1)
            pool.memset(minus_half[:, :], -0.5).then_inc(const_ready, 1)
            pool.wait_ge(const_ready, 3)
            pool.affine_select(out=ident[:, :], in_=ident[:, :], compare_op=ALU.not_equal, fill=1.0, base=0,
                               pattern=[[-1, P]], channel_multiplier=1).then_inc(const_ready, 1)
            pool.wait_ge(const_ready, 4)
            pool.memset(y_out[:, 0, 0:1], 0.0).then_inc(out_free, 16)
            for dst, src in ((w2s_raw[:, :, 0:F], wk[2].rearrange("(f p) n -> p f n", p=P)),
                             (w10_raw[:, :, 0:F], wk[1].rearrange("(f p) n -> p f n", p=P)),
                             (w10_raw[:, :, F:2 * F], wk[0].rearrange("(f p) n -> p f n", p=P)),
                             (kern_raw, kern.rearrange("(f p) n -> p f n", p=P)),
                             (wv_raw, wv.rearrange("(f p) n -> p f n", p=P)),
                             (aw_rep[:, 0, :], aw[0:F, 0].partition_broadcast(P)),
                             (aw_rep[:, 1, :], aw[F:2 * F, 0].partition_broadcast(P)),
                             (bv_rep, bv.partition_broadcast(P)),
                             (bk_rep, bk.partition_broadcast(P)),
                             (bias0[:, :], bias.partition_broadcast(P)),
                             (ab_rep[:, :], ab.partition_broadcast(P))):
                pool.dma_start(dst, src).then_inc(ld_w, 16)

            degrees(0, 0)
            low_adj(0, 0)
            degrees(4, 1)
            root(0, 0, eps0_done, rstd0_done)
            low_adj(4, 1)
            graph(0, 0, first=True)
            with pool.Fori(4, 4 * (G - 4) - 3, 8) as t0:
                for half in range(2):
                    graph(t0 + 4 * half, 1 - half)
            graph(4 * (G - 3), 1)
            graph(4 * (G - 2), 0, ahead=False)
            graph(4 * (G - 1), 1, last=True, ahead=False)
            root(4 * (G - 1), 1, eps1_done, rstd1_done)


_NAMES = ['x', 'adj', 'L0_gnn_kernel', 'L0_gnn_bias', 'L1_gnn_Wv', 'L1_gnn_bv', 'L1_gnn_aw', 'L1_gnn_ab',
          'L1_gnn_Wk', 'L1_gnn_bk']


def kernel(**inputs):
    import numpy as _np
    import concourse.bacc as _bacc
    from concourse import mybir as _mybir
    from concourse.bass_utils import run_bass_kernel_spmd as _run

    nc = _bacc.Bacc("TRN2", target_bir_lowering=False, num_devices=1)
    data = {name: _np.ascontiguousarray(inputs[name]) for name in _NAMES}
    given = [('x', data['x']), ('adj', data['adj']),
             ('adj_t', _np.ascontiguousarray(data['adj'].transpose(0, 2, 1)))]
    given += [(name, data[name]) for name in _NAMES[2:]]
    arrays, args = {}, []
    for name, a in given:
        arrays[f"in_{name}_dram"] = a
        args.append(nc.dram_tensor(f"in_{name}_dram", a.shape, _mybir.dt.from_np(a.dtype), kind="ExternalInput").ap())
    shape = data['x'].shape
    args.append(nc.dram_tensor("out_0_dram", shape, _mybir.dt.float32, kind="ExternalOutput").ap())
    graph_layers(nc, *args)
    r = _run(nc, [arrays], core_ids=[0])
    return r.results[0]["out_0_dram"]
```

```python
from contextlib import ExitStack

import concourse.bass as bass
from concourse import mybir

F32 = mybir.dt.float32
F32R = mybir.dt.float32r
ALU = mybir.AluOpType
ACT = mybir.ActivationFunctionType
AX_X = mybir.AxisListType.X

P = 128
SLOPE = 0.2
NORM_EPS = 1e-5
SUM_EPS = 1e-12


def graph_layers(nc, x, adj, adj_t, kern, bias, wv, bv, aw, ab, wk, bk, out):
    G, N, F = x.shape
    NB = N // P
    FB = F // P
    FS = NB // FB
    NE = F + 2
    S_J, S_I = F, F + 1
    assert NB == 4 and FB == 2 and G % 2 == 0

    x_rows = x.rearrange("g (b p) f -> (g b) p f", p=P)
    adj_rows = adj.rearrange("g (b p) m -> (g b) p m", p=P)
    adj_t_rows = adj_t.rearrange("g (b p) m -> (g b) p m", p=P)
    out_rows = out.rearrange("g (b p) f -> (g b) p f", p=P)

    def graph_of(rows, t):
        return rows[bass.ds(t, NB), :, :].rearrange("b p f -> p b f")

    with ExitStack() as ctx:
        def sb(name, shape, dt=F32):
            return ctx.enter_context(nc.sbuf_tensor(name, shape, dt))

        def sem(name):
            return ctx.enter_context(nc.semaphore(name))

        agg_ps = [ctx.enter_context(nc.psum_tensor(f"agg_ps{f}", [P, N], F32)) for f in range(FB)]
        ring = [ctx.enter_context(nc.psum_tensor(f"ring{i}", [P, 512], F32)) for i in range(NB)]
        turn_ps = [ctx.enter_context(nc.psum_tensor(f"turn_ps{f}", [P, N], F32)) for f in range(FB)]
        target_ps = turn_ps[0]

        def spare_ps(i):
            return agg_ps[i // 2][:, (i % 2) * F:(i % 2 + 1) * F]


        w2s_hi, w2s_lo = sb("w2s_hi", [P, FB, NE], F32R), sb("w2s_lo", [P, FB, NE], F32R)
        w1_hi, w1_lo = sb("w1_hi", [P, FB, F], F32R), sb("w1_lo", [P, FB, F], F32R)
        w0_hi, w0_lo = sb("w0_hi", [P, FB, F], F32R), sb("w0_lo", [P, FB, F], F32R)
        kern_hi, kern_lo = sb("kern_hi", [P, FB, F], F32R), sb("kern_lo", [P, FB, F], F32R)
        bias0 = sb("bias0", [P, F])
        bias1 = sb("bias1", [P, F])
        score_bias = sb("score_bias", [P, 1])
        ident = sb("ident", [P, P])
        ones4 = sb("ones4", [P, NB])
        minus_half = sb("minus_half", [P, NB])

        a_t = [sb(f"a_t{k}", [P, NB, N]) for k in range(2)]
        a_nat = sb("a_nat", [P, NB, N])
        xin = [sb(f"xin{k}", [P, NB, F]) for k in range(2)]
        ah_hi, ah_lo = sb("ah_hi", [P, NB, N], F32R), sb("ah_lo", [P, NB, N], F32R)
        diag = sb("diag", [P, NB, P])
        deg = sb("deg", [P, NB])
        deg1 = sb("deg1", [P, NB])
        dh = [sb(f"dh{k}", [P, NB]) for k in range(2)]
        xd_hi, xd_lo = sb("xd_hi", [P, NB, F], F32R), sb("xd_lo", [P, NB, F], F32R)
        y_hi, y_lo = sb("y_hi", [P, FB, N], F32R), sb("y_lo", [P, FB, N], F32R)
        h0 = sb("h0", [P, NB, F])
        r0 = sb("r0", [P, NB, F])
        x1 = [sb(f"x1_{k}", [P, NB, F]) for k in range(2)]
        x1t_hi, x1t_lo = sb("x1t_hi", [P, FB, N], F32R), sb("x1t_lo", [P, FB, N], F32R)
        score = sb("score", [P, NB, 2])
        sj = sb("sj", [P, NB])
        sj_slope = sb("sj_slope", [P, NB])
        u0 = sb("u0", [P, NB, F])
        u1 = sb("u1", [P, NB, F])
        v2_hi, v2_lo = sb("v2_hi", [P, NB, NE], F32R), sb("v2_lo", [P, NB, F], F32R)
        exp_a = sb("exp_a", [P, NB, N])
        exp_b = sb("exp_b", [P, NB, N])
        s_hi, s_lo = sb("s_hi", [P, NB, N], F32R), sb("s_lo", [P, NB, N], F32R)
        row_sum = sb("row_sum", [P, NB])
        row_inv = sb("row_inv", [P, NB])
        v1 = sb("v1", [P, NB, F])
        v1_hi, v1_lo = sb("v1_hi", [P, NB, F], F32R), sb("v1_lo", [P, NB, F], F32R)
        h1 = sb("h1", [P, NB, F])
        r1 = sb("r1", [P, NB, F])
        y_out = sb("y_out", [P, NB, F])
        stats = [sb(f"stats{k}", [P, NB, 6]) for k in range(2)]
        mean_var = [sb(f"mean_var{k}", [P, NB, 2]) for k in range(2)]
        var_eps = [sb(f"var_eps{k}", [P, NB]) for k in range(2)]
        rstd = [sb(f"rstd{k}", [P, NB]) for k in range(2)]
        shift = [sb(f"shift{k}", [P, NB]) for k in range(2)]
        pace = sb("pace", [P, 1])

        w2s_raw = exp_a[:, 0:2, :].rearrange("p b n -> p (b n)")[:, 0:FB * NE].rearrange("p (f n) -> p f n", f=FB)
        w1_raw = exp_b[:, 0, :].rearrange("p (f n) -> p f n", f=FB)
        w0_raw = exp_b[:, 1, :].rearrange("p (f n) -> p f n", f=FB)
        wv_raw = exp_a[:, 2, :].rearrange("p (f n) -> p f n", f=FB)
        kern_raw = exp_a[:, 3, :].rearrange("p (f n) -> p f n", f=FB)
        aw_rep = exp_b[:, 2, :].rearrange("p (k n) -> p k n", k=2)
        bv_rep = exp_b[:, 3, 0:F]
        dots = exp_b[:, 3, F:2 * F]
        bk_rep = h1[:, 0:3, :]
        ab_rep = sb("ab_rep", [P, 1])
        bv_dot = sb("bv_dot", [P, 2])

        ld_kernel = sem("ld_kernel")
        ld_w = sem("ld_w")
        ld_rep = sem("ld_rep")
        ld_at = [sem(f"ld_at{k}") for k in range(2)]
        ld_x = [sem(f"ld_x{k}") for k in range(2)]
        ld_nat = sem("ld_nat")
        out_free = sem("out_free")
        const_ready = sem("const_ready")
        set_dve = sem("set_dve")
        kernel_ready = sem("kernel_ready")
        weights_ready = sem("weights_ready")
        agg_done = sem("agg_done")
        kern_done = sem("kern_done")
        turn_done = sem("turn_done")
        u2_done = sem("u2_done")
        uw1_done = sem("uw1_done")
        uw0_done = sem("uw0_done")
        target_done = sem("target_done")
        sv2_done = sem("sv2_done")
        sv1_done = sem("sv1_done")
        ah_hi_done = sem("ah_hi_done")
        xd_hi_done = sem("xd_hi_done")
        y_hi_done = sem("y_hi_done")
        x1t_hi_done = sem("x1t_hi_done")
        v2_hi_done = sem("v2_hi_done")
        u1_done = sem("u1_done")
        u0_done = sem("u0_done")
        x1_done = sem("x1_done")
        exp_done = sem("exp_done")
        s_hi_done = sem("s_hi_done")
        v1_hi_done = sem("v1_hi_done")
        out_done = sem("out_done")
        xd_lo_done = sem("xd_lo_done")
        y_lo_done = sem("y_lo_done")
        h0_done = sem("h0_done")
        r0_done = sem("r0_done")
        stat0_done = sem("stat0_done")
        agr0_done = sem("agr0_done")
        eps0_done = sem("eps0_done")
        shift0_done = sem("shift0_done")
        x1t_lo_done = sem("x1t_lo_done")
        score_done = sem("score_done")
        sj_done = sem("sj_done")
        v2_lo_done = sem("v2_lo_done")
        max_done = sem("max_done")
        s_lo_done = sem("s_lo_done")
        sum_done = sem("sum_done")
        inv_done = sem("inv_done")
        v1_done = sem("v1_done")
        v1_lo_done = sem("v1_lo_done")
        h1_done = sem("h1_done")
        r1_done = sem("r1_done")
        stat1_done = sem("stat1_done")
        agr1_done = sem("agr1_done")
        eps1_done = sem("eps1_done")
        shift1_done = sem("shift1_done")
        deg_done = sem("deg_done")
        deg1_done = sem("deg1_done")
        dh_done = sem("dh_done")
        diag_done = sem("diag_done")
        s_done = sem("s_done")
        low_done = sem("low_done")
        ah_lo_done = sem("ah_lo_done")
        u0_bias_done = sem("u0_bias_done")
        rstd0_done = sem("rstd0_done")
        rstd1_done = sem("rstd1_done")

        def loaded(k, t):
            return t * 2 + (16 if k == 0 else 8)

        def loaded_at(k, t):
            return t * 8 + (64 if k == 0 else 32)

        def diagonal(tensor, width):
            full = tensor[:, 0, 0:P]
            return bass.AP(full.tensor, full.offset, [list(full.ap[0]), [width + P, NB], [1, P]])

        on_diagonal = ident[:, :].unsqueeze(1).to_broadcast([P, NB, P])

        block = ctx.enter_context(nc.Block())

        @block.sync
        def _(sp):
            def load_x(t, k):
                sp.dma_start(xin[k][:, :, :], graph_of(x_rows, t)).then_inc(ld_x[k], 16)

            def load_nat(t):
                sp.dma_start(a_nat[:, :, :], graph_of(adj_rows, t)).then_inc(ld_nat, 16)

            def load_at_block(t, k, j):
                sp.dma_start(a_t[k][:, j, :], adj_t_rows[bass.ds(t + j, 1), :, :].rearrange("b p f -> p (b f)"))\
                  .then_inc(ld_at[k], 16)

            def load_at(t, k):
                for j in range(NB):
                    load_at_block(t, k, j)

            def store(t):
                sp.wait_ge(out_done, t + 4)
                sp.dma_start(graph_of(out_rows, t), y_out[:, :, :]).then_inc(out_free, 16)

            def ahead(t, k):
                sp.wait_ge(x1_done, t + 4)
                load_x(t + 8, k)
                sp.wait_ge(deg_done, t + 8)
                load_nat(t + 8)
                for j in range(NB):
                    sp.wait_ge(s_done, t + j + 1)
                    load_at_block(t + 8, k, j)

            def load_weights(dst, w, landed):
                sp.dma_start(dst, w.rearrange("(f p) n -> p f n", p=P)).then_inc(landed, 16)

            load_nat(0)
            load_at(0, 0)
            load_x(0, 0)
            load_weights(kern_raw, kern, ld_kernel)
            load_weights(wv_raw, wv, ld_w)
            load_weights(w2s_raw[:, :, 0:F], wk[2], ld_w)
            load_weights(w1_raw, wk[1], ld_w)
            load_weights(w0_raw, wk[0], ld_w)
            sp.wait_ge(deg_done, 4)
            load_nat(4)
            load_x(4, 1)
            load_at(4, 1)
            ahead(0, 0)
            with sp.Fori(4, 4 * (G - 4) - 3, 8) as t0:
                for half in range(2):
                    t = t0 + 4 * half
                    ahead(t, 1 - half)
                    store(t - 4)
            ahead(4 * (G - 3), 1)
            for g in range(G - 4, G):
                store(4 * g)
            sp.wait_ge(out_free, 16 * (G + 1))

        @block.tensor
        def _(pe):
            def three_passes(dst, terms, start=True, stop=True):
                for n, (l_hi, l_lo, r_hi, r_lo) in enumerate(terms):
                    pe.matmul(dst[:, 0:r_hi.shape[-1]], l_hi, r_hi, start=(start and n == 0), stop=False)
                    pe.matmul(dst[:, 0:r_lo.shape[-1]], l_hi, r_lo, start=False, stop=False)
                    last = pe.matmul(dst[:, 0:r_hi.shape[-1]], l_lo, r_hi, start=False,
                                     stop=(stop and n == len(terms) - 1))
                return last

            def aggregate(t, between=None, first=False):
                pe.wait_ge(ah_lo_done, t + 4)
                pe.wait_ge(xd_lo_done, t + 4)
                for f in range(FB):
                    if not first:
                        pe.wait_ge(y_lo_done, t - 4 + FS * (f + 1))
                    cols = slice(f * P, (f + 1) * P)
                    terms = [(xd_hi[:, j, cols], xd_lo[:, j, cols], ah_hi[:, j, :], ah_lo[:, j, :])
                             for j in range(NB)]
                    if f == 0:
                        three_passes(agg_ps[f], terms[:1], stop=False)
                        if between:
                            between()
                        last = three_passes(agg_ps[f], terms[1:], start=False)
                    else:
                        last = three_passes(agg_ps[f], terms)
                    last.then_inc(agg_done, FS)

            def times_kernel(t, first=False):
                pe.wait_ge(y_lo_done, t + 4)
                for i in range(NB):
                    if not first:
                        pe.wait_ge(u1_done, t - 4 + i + 1)
                    rows = slice(i * P, (i + 1) * P)
                    three_passes(ring[i], [(y_hi[:, f, rows], y_lo[:, f, rows], kern_hi[:, f, :], kern_lo[:, f, :])
                                           for f in range(FB)]).then_inc(kern_done, 1)

            def turn_x1(t, k, first=False):
                pe.wait_ge(x1_done, t + 4)
                for f in range(FB):
                    if not first:
                        pe.wait_ge(exp_done if f == 0 else x1t_lo_done, t)
                    for i in range(NB):
                        last = pe.transpose(turn_ps[f][:, i * P:(i + 1) * P], x1[k][:, i, f * P:(f + 1) * P],
                                            ident[:, :])
                    last.then_inc(turn_done, FS)

            def x1_rows(f, i):
                rows = slice(i * P, (i + 1) * P)
                return x1t_hi[:, f, rows], x1t_lo[:, f, rows]

            def times_w2(t, first=False):
                pe.wait_ge(x1t_lo_done, t + 4)
                for i in range(NB):
                    pe.wait_ge(h0_done if first else h1_done, (t + 4 if first else t) - 4 + i + 1)
                    three_passes(ring[i], [(*x1_rows(f, i), w2s_hi[:, f, :], w2s_lo[:, f, :]) for f in range(FB)])\
                        .then_inc(u2_done, 1)

            def times_w1(t):
                for i in range(NB):
                    pe.wait_ge(v2_lo_done, t + i + 1)
                    three_passes(ring[i], [(*x1_rows(f, i), w1_hi[:, f, :], w1_lo[:, f, :]) for f in range(FB)])\
                        .then_inc(uw1_done, 1)

            def times_w0(t, last=False):
                for i in range(NB):
                    if last:
                        dst = spare_ps(i)
                    else:
                        pe.wait_ge(v1_done, t + i + 1)
                        dst = ring[i]
                    three_passes(dst, [(*x1_rows(f, i), w0_hi[:, f, :], w0_lo[:, f, :]) for f in range(FB)])\
                        .then_inc(uw0_done, 1)

            def spread_targets(t):
                pe.wait_ge(score_done, t + 4)
                for i in range(NB):
                    last = pe.transpose(target_ps[:, i * P:(i + 1) * P],
                                        score[:, i, 1:2].to_broadcast([P, P]), ident[:, :])
                last.then_inc(target_done, 4)

            def times_s_v2(t):
                pe.wait_ge(s_lo_done, t + 4)
                for i in range(NB):
                    pe.wait_ge(h0_done, t + 4 + i + 1)
                    rows = slice(i * P, (i + 1) * P)
                    three_passes(ring[i], [(s_hi[:, j, rows], s_lo[:, j, rows], v2_hi[:, j, :], v2_lo[:, j, :])
                                           for j in range(NB)]).then_inc(sv2_done, 1)

            def times_s_v2_by_source(t):
                for j in range(NB):
                    pe.wait_ge(s_lo_done, t + j + 1)
                    for i in range(NB):
                        if j == 0:
                            pe.wait_ge(u1_done, t + i + 1)
                        rows = slice(i * P, (i + 1) * P)
                        done = three_passes(ring[i], [(s_hi[:, j, rows], s_lo[:, j, rows], v2_hi[:, j, :], v2_lo[:, j, :])],
                                            start=(j == 0), stop=(j == NB - 1))
                        if j == NB - 1:
                            done.then_inc(sv2_done, 1)

            def times_s_v1(t, i, last=False):
                if i == 0:
                    pe.wait_ge(v1_lo_done, t + 4)
                if not last:
                    pe.wait_ge(u0_done, t + i + 1)
                rows = slice(i * P, (i + 1) * P)
                three_passes(ring[i], [(s_hi[:, j, rows], s_lo[:, j, rows], v1_hi[:, j, :], v1_lo[:, j, :])
                                       for j in range(NB)]).then_inc(sv1_done, 1)

            def graph(t, k, first=False, last=False):
                times_w2(t, first)
                if last:
                    spread_targets(t)
                else:
                    aggregate(t + 4, between=lambda: spread_targets(t))
                times_w1(t)
                if not last:
                    times_kernel(t + 4)
                if last:
                    times_w0(t, last)
                    times_s_v2_by_source(t)
                else:
                    times_s_v2(t)
                    times_w0(t)
                for i in range(NB):
                    times_s_v1(t, i, last)
                    if i == 1 and not last:
                        turn_x1(t + 4, 1 - k)

            pe.wait_ge(const_ready, 4)
            aggregate(0, first=True)
            pe.wait_ge(kernel_ready, 1)
            times_kernel(0, first=True)
            turn_x1(0, 0, first=True)
            pe.wait_ge(weights_ready, 1)
            graph(0, 0, first=True)
            with pe.Fori(4, 4 * (G - 2) - 3, 8) as t0:
                for half in range(2):
                    graph(t0 + 4 * half, 1 - half)
            graph(4 * (G - 1), 1, last=True)

        @block.scalar
        def _(act):
            def high_adj(t, k, first=False):
                act.wait_ge(ld_at[k], loaded_at(k, t))
                if not first:
                    act.wait_ge(agg_done, t)
                act.activation(ah_hi[:, :, :], a_t[k][:, :, :], ACT.Copy).then_inc(ah_hi_done, 4)

            def row_sums(t):
                act.wait_ge(ld_nat, t * 4 + 16)
                for i in range(NB):
                    act.activation(a_nat[:, i, :], a_nat[:, i, :], ACT.Copy, accum_out=deg[:, i:i + 1])\
                       .then_inc(deg_done, 1)

            def high_xd(t, k, first=False):
                act.wait_ge(ld_x[k], loaded(k, t))
                act.wait_ge(dh_done, t + 4)
                if not first:
                    act.wait_ge(agg_done, t)
                for i in range(NB):
                    act.activation(xd_hi[:, i, :], xin[k][:, i, :], ACT.Copy, scale=dh[k][:, i:i + 1])\
                       .then_inc(xd_hi_done, 1)

            def high_y(t, f):
                act.wait_ge(agg_done, t + FS * (f + 1))
                act.activation(y_hi[:, f, :], agg_ps[f][:, :], ACT.Copy).then_inc(y_hi_done, FS)

            def high_x1t(t):
                for f in range(FB):
                    act.wait_ge(turn_done, t + FS * (f + 1))
                    act.activation(x1t_hi[:, f, :], turn_ps[f][:, :], ACT.Copy).then_inc(x1t_hi_done, FS)

            def high_v2(t):
                for i in range(NB):
                    act.wait_ge(score_done, t + i + 1)
                    act.activation(v2_hi[:, i, 0:F], ring[i][:, 0:F], ACT.Copy).then_inc(v2_hi_done, 1)

            def take_u1(t, i):
                act.wait_ge(uw1_done, t + i + 1)
                act.activation(u1[:, i, :], ring[i][:, 0:F], ACT.Copy).then_inc(u1_done, 1)

            def take_u0(t, i, last=False):
                act.wait_ge(uw0_done, t + 2 * (i // 2 + 1) if last else t + i + 1)
                act.activation(u0[:, i, :], spare_ps(i) if last else ring[i][:, 0:F], ACT.Copy).then_inc(u0_done, 1)

            def norm_x1(t, k, i):
                if i == 0:
                    act.wait_ge(shift0_done, t + 4)
                act.activation(x1[k][:, i, :], r0[:, i, :], ACT.Identity, scale=rstd[0][:, i:i + 1],
                               bias=shift[0][:, i:i + 1]).then_inc(x1_done, 1)

            def exps(t, j):
                if j == 0:
                    act.wait_ge(target_done, t + 4)
                    act.wait_ge(sj_done, t + 4)
                act.activation(exp_a[:, j, :], target_ps[:, :], ACT.Exp, bias=sj[:, j:j + 1])
                act.activation(exp_b[:, j, :], target_ps[:, :], ACT.Exp, bias=sj_slope[:, j:j + 1], scale=SLOPE)\
                   .then_inc(exp_done, 1)

            def high_s(t, j):
                act.wait_ge(s_done, t + j + 1)
                act.activation(s_hi[:, j, :], exp_b[:, j, :], ACT.Copy).then_inc(s_hi_done, 1)

            def high_v1(t, i, n):
                act.wait_ge(v1_done, t + i + n)
                act.activation(v1_hi[:, i:i + n, :], v1[:, i:i + n, :], ACT.Copy).then_inc(v1_hi_done, n)

            def norm_out(t, first_block):
                if first_block == 0:
                    act.wait_ge(shift1_done, t + 4)
                    act.wait_ge(out_free, t * 4 + 16)
                for i in range(first_block, first_block + 2):
                    act.activation(y_out[:, i, :], r1[:, i, :], ACT.Identity, scale=rstd[1][:, i:i + 1],
                                   bias=shift[1][:, i:i + 1]).then_inc(out_done, 1)

            def graph(t, k, first=False, last=False, ahead=True):
                high_v2(t)
                for j in range(NB - 1):
                    exps(t, j)
                if not last:
                    high_y(t + 4, 0)
                exps(t, NB - 1)
                if not last:
                    high_y(t + 4, 1)
                high_s(t, 0)
                high_s(t, 1)
                take_u1(t, 0)
                take_u1(t, 1)
                high_s(t, 2)
                high_s(t, 3)
                take_u1(t, 2)
                take_u1(t, 3)
                if ahead:
                    row_sums(t + 8)
                    high_adj(t + 8, k)
                    high_xd(t + 8, k)
                high_v1(t, 0, 2)
                if not last:
                    norm_x1(t + 4, 1 - k, 0)
                high_v1(t, 2, 1)
                if not last:
                    norm_x1(t + 4, 1 - k, 1)
                high_v1(t, 3, 1)
                take_u0(t, 0, last)
                if not last:
                    norm_x1(t + 4, 1 - k, 2)
                take_u0(t, 1, last)
                if not last:
                    norm_x1(t + 4, 1 - k, 3)
                take_u0(t, 2, last)
                take_u0(t, 3, last)
                if not first:
                    norm_out(t - 4, 0)
                if not last:
                    high_x1t(t + 4)
                if not first:
                    norm_out(t - 4, 2)

            row_sums(0)
            for dst, src in ((aw_rep[:, 0, :], aw[0:F, 0]), (aw_rep[:, 1, :], aw[F:2 * F, 0]), (bv_rep, bv),
                             (bk_rep, bk), (bias0[:, :], bias), (ab_rep[:, :], ab)):
                act.dma_start(dst, src.partition_broadcast(P)).then_inc(ld_rep, 16)
            high_xd(0, 0, first=True)
            row_sums(4)
            high_y(0, 0)
            high_y(0, 1)
            high_adj(4, 1)
            for i in range(NB):
                norm_x1(0, 0, i)
            high_x1t(0)
            high_xd(4, 1)
            graph(0, 0, first=True)
            with act.Fori(4, 4 * (G - 4) - 3, 8) as t0:
                for half in range(2):
                    graph(t0 + 4 * half, 1 - half)
            graph(4 * (G - 3), 1)
            graph(4 * (G - 2), 0, ahead=False)
            graph(4 * (G - 1), 1, last=True, ahead=False)
            norm_out(4 * (G - 1), 0)
            norm_out(4 * (G - 1), 2)

        @block.vector
        def _(dve):
            def low_xd(t, k, first_block):
                for i in range(first_block, first_block + 2):
                    dve.wait_ge(xd_hi_done, t + i + 1)
                    dve.scalar_tensor_tensor(xd_lo[:, i, :], xin[k][:, i, :], dh[k][:, i:i + 1],
                                             xd_hi[:, i, :].bitcast(F32), ALU.mult, ALU.subtract)\
                       .then_inc(xd_lo_done, 1)

            def low_y(t, f):
                dve.wait_ge(y_hi_done, t + FS * (f + 1))
                dve.tensor_tensor(y_lo[:, f, :], agg_ps[f][:, :], y_hi[:, f, :].bitcast(F32), ALU.subtract)\
                   .then_inc(y_lo_done, FS)

            def layer0_out(t, k, i):
                dve.wait_ge(kern_done, t + i + 1)
                dve.scalar_tensor_tensor(h0[:, i, :], ring[i][:, 0:F], dh[k][:, i:i + 1], bias0[:, :],
                                         ALU.mult, ALU.add).then_inc(h0_done, 1)

            def residual0(t, k, i):
                dve.wait_ge(h0_done, t + i + 1)
                dve.scalar_tensor_tensor(r0[:, i, :], h0[:, i, :], 0.0, xin[k][:, i, :],
                                         ALU.max, ALU.add).then_inc(r0_done, 1)

            def layer0_stats(t, i):
                dve.wait_ge(r0_done, t + i + 1)
                dve.bn_stats(stats[0][:, i, :], r0[:, i, :]).then_inc(stat0_done, 1)

            def moments(t, layer, stat_done, agr_done):
                dve.wait_ge(stat_done, t + 4)
                dve.memset(pace[:, :], 0.0)
                for i in range(NB):
                    dve.bn_aggr(mean_var[layer][:, i, :], stats[layer][:, i, :]).then_inc(agr_done, 1)

            def add_eps(t, layer, agr_done, eps_done):
                dve.wait_ge(agr_done, t + 4)
                dve.tensor_scalar(var_eps[layer][:, :], mean_var[layer][:, :, 1], NORM_EPS, None, ALU.add)\
                   .then_inc(eps_done, 4)

            def low_x1t(t):
                for f in range(FB):
                    dve.wait_ge(x1t_hi_done, t + FS * (f + 1))
                    dve.tensor_tensor(x1t_lo[:, f, :], turn_ps[f][:, :], x1t_hi[:, f, :].bitcast(F32), ALU.subtract)\
                       .then_inc(x1t_lo_done, FS)

            def take_v2(t):
                for s in range(NB + 1):
                    if s == NB:
                        source_scores(t)
                    if s < NB:
                        dve.wait_ge(u2_done, t + s + 1)
                        dve.tensor_copy(score[:, s, :], ring[s][:, S_J:S_I + 1]).then_inc(score_done, 1)
                    if s >= 1:
                        i = s - 1
                        dve.wait_ge(v2_hi_done, t + i + 1)
                        dve.tensor_tensor(v2_lo[:, i, :], ring[i][:, 0:F], v2_hi[:, i, 0:F].bitcast(F32),
                                          ALU.subtract).then_inc(v2_lo_done, 1)

            def source_scores(t):
                dve.wait_ge(score_done, t + 4)
                dve.tensor_scalar(sj[:, :], score[:, :, 0], score_bias[:, 0:1], None, ALU.add).then_inc(sj_done, 2)
                dve.tensor_scalar(sj_slope[:, :], score[:, :, 0], score_bias[:, 0:1], SLOPE, ALU.add, ALU.mult)\
                   .then_inc(sj_done, 2)

            def larger_exp(t, j):
                dve.wait_ge(exp_done, t + j + 1)
                dve.tensor_tensor(exp_a[:, j, :], exp_a[:, j, :], exp_b[:, j, :], ALU.max).then_inc(max_done, 1)

            def low_s(t, j):
                dve.wait_ge(s_hi_done, t + j + 1)
                dve.tensor_tensor(s_lo[:, j, :], exp_b[:, j, :], s_hi[:, j, :].bitcast(F32), ALU.subtract)\
                   .then_inc(s_lo_done, 1)

            def sum_rows(t, i):
                dve.wait_ge(sv2_done, t + i + 1)
                dve.tensor_scalar(row_sum[:, i:i + 1], ring[i][:, F:F + 1], SUM_EPS, None, ALU.add)\
                   .then_inc(sum_done, 1)

            def invert_rows(t, i):
                dve.wait_ge(sum_done, t + i + 1)
                dve.reciprocal(row_inv[:, i:i + 1], row_sum[:, i:i + 1]).then_inc(inv_done, 1)

            def make_v1(t, i):
                dve.wait_ge(inv_done, t + i + 1)
                dve.scalar_tensor_tensor(v1[:, i, :], ring[i][:, 0:F], row_inv[:, i:i + 1], u1[:, i, :],
                                         ALU.mult, ALU.add).then_inc(v1_done, 1)

            def low_v1(t, i, n):
                dve.wait_ge(v1_hi_done, t + i + n)
                dve.tensor_tensor(v1_lo[:, i:i + n, :], v1[:, i:i + n, :], v1_hi[:, i:i + n, :].bitcast(F32),
                                  ALU.subtract).then_inc(v1_lo_done, n)

            def make_h1(t, i):
                dve.wait_ge(sv1_done, t + i + 1)
                dve.wait_ge(u0_bias_done, t + i + 1)
                dve.scalar_tensor_tensor(h1[:, i, :], ring[i][:, 0:F], row_inv[:, i:i + 1], u0[:, i, :],
                                         ALU.mult, ALU.add).then_inc(h1_done, 1)

            def layer1_out(t, k):
                dve.wait_ge(h1_done, t + 4)
                dve.scalar_tensor_tensor(r1[:, :, :], h1[:, :, :], 0.0, x1[k][:, :, :], ALU.max, ALU.add)\
                   .then_inc(r1_done, 4)

            def layer1_out_block(t, k, i):
                dve.wait_ge(h1_done, t + i + 1)
                dve.scalar_tensor_tensor(r1[:, i, :], h1[:, i, :], 0.0, x1[k][:, i, :], ALU.max, ALU.add)\
                   .then_inc(r1_done, 1)

            def layer1_stats(t, i, n=2):
                if i == 0 or n == 1:
                    dve.wait_ge(r1_done, t + 4 if n == 2 else t + i + 1)
                for m in range(i, i + n):
                    dve.bn_stats(stats[1][:, m, :], r1[:, m, :]).then_inc(stat1_done, 1)

            def shift_by(t, layer, rstd_done, shift_done):
                dve.wait_ge(rstd_done, t + 4)
                dve.scalar_tensor_tensor(shift[layer][:, :], mean_var[layer][:, :, 0], -1.0, rstd[layer][:, :],
                                         ALU.mult, ALU.mult).then_inc(shift_done, 4)

            def graph(t, k, first=False, last=False, ahead=True):
                take_v2(t)
                if not first:
                    layer1_out(t - 4, 1 - k)
                larger_exp(t, 0)
                if not first:
                    layer1_stats(t - 4, 0)
                larger_exp(t, 1)
                if not first:
                    layer1_stats(t - 4, 2)
                larger_exp(t, 2)
                if not last:
                    low_y(t + 4, 0)
                larger_exp(t, 3)
                if not first:
                    moments(t - 4, 1, stat1_done, agr1_done)
                if not last:
                    low_y(t + 4, 1)
                low_s(t, 0)
                if not first:
                    add_eps(t - 4, 1, agr1_done, eps1_done)
                for j in range(1, NB):
                    low_s(t, j)
                if not last:
                    layer0_out(t + 4, 1 - k, 0)
                    layer0_out(t + 4, 1 - k, 1)
                    residual0(t + 4, 1 - k, 0)
                    layer0_out(t + 4, 1 - k, 2)
                    residual0(t + 4, 1 - k, 1)
                    layer0_stats(t + 4, 0)
                    layer0_out(t + 4, 1 - k, 3)
                    residual0(t + 4, 1 - k, 2)
                    layer0_stats(t + 4, 1)
                    sum_rows(t, 0)
                    residual0(t + 4, 1 - k, 3)
                    invert_rows(t, 0)
                    layer0_stats(t + 4, 2)
                    make_v1(t, 0)
                    layer0_stats(t + 4, 3)
                    sum_rows(t, 1)
                    moments(t + 4, 0, stat0_done, agr0_done)
                    invert_rows(t, 1)
                    add_eps(t + 4, 0, agr0_done, eps0_done)
                    make_v1(t, 1)
                else:
                    for i in range(2):
                        sum_rows(t, i)
                        invert_rows(t, i)
                        make_v1(t, i)
                sum_rows(t, 2)
                invert_rows(t, 2)
                make_v1(t, 2)
                if not last:
                    shift_by(t + 4, 0, rstd0_done, shift0_done)
                low_v1(t, 0, 2)
                sum_rows(t, 3)
                invert_rows(t, 3)
                make_v1(t, 3)
                low_v1(t, 2, 1)
                low_v1(t, 3, 1)
                if not first:
                    shift_by(t - 4, 1, rstd1_done, shift1_done)
                if ahead:
                    low_xd(t + 8, k, 0)
                    low_xd(t + 8, k, 2)
                make_h1(t, 0)
                make_h1(t, 1)
                if last:
                    dve.wait_ge(out_done, t)
                    layer1_out_block(t, k, 0)
                    layer1_stats(t, 0, 1)
                    layer1_out_block(t, k, 1)
                else:
                    low_x1t(t + 4)
                make_h1(t, 2)
                if last:
                    layer1_stats(t, 1, 1)
                    layer1_out_block(t, k, 2)
                    layer1_stats(t, 2, 1)
                make_h1(t, 3)
                if last:
                    layer1_out_block(t, k, 3)
                    layer1_stats(t, 3, 1)

            dve.memset(v2_hi[:, :, F:F + 1].bitcast(F32), 1.0)
            dve.memset(v2_hi[:, :, F + 1:F + 2].bitcast(F32), 0.0)
            dve.wait_ge(ld_at[0], loaded_at(0, 0))
            dve.tensor_copy(ah_hi[:, :, :], a_t[0][:, :, :]).then_inc(ah_hi_done, 4)
            dve.wait_ge(const_ready, 4)
            dve.tensor_tensor(diag[:, :, :], diagonal(a_t[0], N), on_diagonal, ALU.add).then_inc(diag_done, 2)
            dve.wait_ge(ah_hi_done, 4)
            dve.tensor_tensor(ah_lo[:, :, :], a_t[0][:, :, :], ah_hi[:, :, :].bitcast(F32), ALU.subtract)\
               .then_inc(low_done, 4)
            dve.wait_ge(diag_done, 2)
            dve.wait_ge(low_done, 4)
            dve.tensor_copy(diagonal(ah_hi, N), diag[:, :, :]).then_inc(diag_done, 2)
            dve.wait_ge(diag_done, 4)
            dve.tensor_tensor(diagonal(ah_lo, N), diag[:, :, :], diagonal(ah_hi, N).bitcast(F32), ALU.subtract)\
               .then_inc(ah_lo_done, 4)
            low_xd(0, 0, 0)
            low_xd(0, 0, 2)
            dve.wait_ge(ld_kernel, 16)
            dve.tensor_copy(kern_hi[:, :, :], kern_raw).then_inc(set_dve, 1)
            dve.wait_ge(set_dve, 1)
            dve.tensor_tensor(kern_lo[:, :, :], kern_raw, kern_hi[:, :, :].bitcast(F32), ALU.subtract)\
               .then_inc(kernel_ready, 1)
            dve.wait_ge(ld_rep, 16 * 6)
            dve.wait_ge(ld_w, 16 * 4)
            done = 1
            for c in range(2):
                for f in range(FB):
                    dve.tensor_tensor_reduce(dots, wv_raw[:, f, :], aw_rep[:, c, :], 1.0, 0.0, ALU.mult, ALU.add,
                                             w2s_raw[:, f, F + c:F + c + 1]).then_inc(set_dve, 1)
                    done += 1
                    dve.wait_ge(set_dve, done)
                dve.tensor_tensor_reduce(dots, bv_rep, aw_rep[:, c, :], 1.0, 0.0, ALU.mult, ALU.add,
                                         bv_dot[:, c:c + 1]).then_inc(set_dve, 1)
                done += 1
                dve.wait_ge(set_dve, done)
            dve.scalar_tensor_tensor(score_bias[:, :], bv_dot[:, 0:1], ab_rep[:, :], bv_dot[:, 1:2],
                                     ALU.add, ALU.add)
            dve.tensor_tensor(bias1[:, :], bk_rep[:, 0, :], bk_rep[:, 1, :], ALU.add)
            for hi, raw in ((w2s_hi, w2s_raw), (w1_hi, w1_raw), (w0_hi, w0_raw)):
                split = dve.tensor_copy(hi[:, :, :], raw)
            split.then_inc(set_dve, 1)
            done += 1
            low_y(0, 0)
            dve.wait_ge(set_dve, done)
            dve.tensor_tensor(bias1[:, :], bias1[:, :], bk_rep[:, 2, :], ALU.add)
            for lo, raw, hi in ((w2s_lo, w2s_raw, w2s_hi), (w1_lo, w1_raw, w1_hi), (w0_lo, w0_raw, w0_hi)):
                split = dve.tensor_tensor(lo[:, :, :], raw, hi[:, :, :].bitcast(F32), ALU.subtract)
            split.then_inc(weights_ready, 1)
            low_y(0, 1)
            for s in range(NB + 2):
                if s < NB:
                    layer0_out(0, 0, s)
                if 1 <= s <= NB:
                    residual0(0, 0, s - 1)
                if s >= 2:
                    layer0_stats(0, s - 2)
            moments(0, 0, stat0_done, agr0_done)
            add_eps(0, 0, agr0_done, eps0_done)
            shift_by(0, 0, rstd0_done, shift0_done)
            low_x1t(0)
            low_xd(4, 1, 0)
            low_xd(4, 1, 2)
            dve.wait_ge(weights_ready, 1)
            graph(0, 0, first=True)
            with dve.Fori(4, 4 * (G - 4) - 3, 8) as t0:
                for half in range(2):
                    graph(t0 + 4 * half, 1 - half)
            graph(4 * (G - 3), 1)
            graph(4 * (G - 2), 0, ahead=False)
            graph(4 * (G - 1), 1, last=True, ahead=False)
            moments(4 * (G - 1), 1, stat1_done, agr1_done)
            add_eps(4 * (G - 1), 1, agr1_done, eps1_done)
            shift_by(4 * (G - 1), 1, rstd1_done, shift1_done)

        @block.gpsimd
        def _(pool):
            def make_s(t, k, j):
                if j == 0:
                    pool.wait_ge(ld_at[k], loaded_at(k, t))
                pool.wait_ge(max_done, t + j + 1)
                pool.tensor_tensor(exp_b[:, j, :], a_t[k][:, j, :], exp_a[:, j, :], ALU.mult).then_inc(s_done, 1)

            def degrees(t, k):
                pool.wait_ge(deg_done, t + 4)
                pool.tensor_tensor(deg1[:, :], deg[:, :], ones4[:, :], ALU.add).then_inc(deg1_done, 4)
                pool.wait_ge(deg1_done, t + 4)
                pool.tensor_tensor(dh[k][:, :], deg1[:, :], minus_half[:, :], ALU.pow).then_inc(dh_done, 4)

            def split_diagonal(t, k):
                pool.wait_ge(ah_hi_done, t + 4)
                pool.tensor_tensor(diagonal(ah_hi, N), diagonal(a_t[k], N), on_diagonal, ALU.add)\
                    .then_inc(diag_done, 2)
                pool.tensor_tensor(diag[:, :, :], diagonal(a_t[k], N), on_diagonal, ALU.add).then_inc(diag_done, 2)

            def low_adj(t, k, j):
                if j == 0:
                    pool.wait_ge(diag_done, t + 4)
                pool.tensor_tensor(ah_lo[:, j, :], a_t[k][:, j, :], ah_hi[:, j, :].bitcast(F32), ALU.subtract)\
                    .then_inc(low_done, 1)
                if j == NB - 1:
                    pool.wait_ge(low_done, t + 4)
                    pool.tensor_tensor(diagonal(ah_lo, N), diag[:, :, :], diagonal(ah_hi, N).bitcast(F32),
                                       ALU.subtract).then_inc(ah_lo_done, 4)

            def add_bias(t, i):
                pool.wait_ge(u0_done, t + i + 1)
                pool.tensor_tensor(u0[:, i, :], u0[:, i, :], bias1[:, :], ALU.add).then_inc(u0_bias_done, 1)

            def root(t, layer, eps_done, rstd_done):
                pool.wait_ge(eps_done, t + 4)
                pool.tensor_tensor(rstd[layer][:, :], var_eps[layer][:, :], minus_half[:, :], ALU.pow)\
                    .then_inc(rstd_done, 4)

            def graph(t, k, first=False, last=False, ahead=True):
                for j in range(NB):
                    make_s(t, k, j)
                if not first:
                    root(t - 4, 1, eps1_done, rstd1_done)
                if ahead:
                    degrees(t + 8, k)
                if not last:
                    root(t + 4, 0, eps0_done, rstd0_done)
                if ahead:
                    split_diagonal(t + 8, k)
                for i in range(NB):
                    add_bias(t, i)
                    if ahead:
                        low_adj(t + 8, k, i)

            pool.memset(ident[:, :], 0.0).then_inc(const_ready, 1)
            pool.memset(ones4[:, :], 1.0).then_inc(const_ready, 1)
            pool.memset(minus_half[:, :], -0.5).then_inc(const_ready, 1)
            pool.wait_ge(const_ready, 3)
            pool.affine_select(out=ident[:, :], in_=ident[:, :], compare_op=ALU.not_equal, fill=1.0, base=0,
                               pattern=[[-1, P]], channel_multiplier=1).then_inc(const_ready, 1)
            pool.wait_ge(const_ready, 4)
            pool.memset(y_out[:, 0, 0:1], 0.0).then_inc(out_free, 16)
            degrees(0, 0)
            degrees(4, 1)
            split_diagonal(4, 1)
            root(0, 0, eps0_done, rstd0_done)
            for j in range(NB):
                low_adj(4, 1, j)
            pool.wait_ge(weights_ready, 1)
            graph(0, 0, first=True)
            with pool.Fori(4, 4 * (G - 4) - 3, 8) as t0:
                for half in range(2):
                    graph(t0 + 4 * half, 1 - half)
            graph(4 * (G - 3), 1)
            graph(4 * (G - 2), 0, ahead=False)
            graph(4 * (G - 1), 1, last=True, ahead=False)
            root(4 * (G - 1), 1, eps1_done, rstd1_done)


_NAMES = ['x', 'adj', 'L0_gnn_kernel', 'L0_gnn_bias', 'L1_gnn_Wv', 'L1_gnn_bv', 'L1_gnn_aw', 'L1_gnn_ab',
          'L1_gnn_Wk', 'L1_gnn_bk']


def kernel(**inputs):
    import numpy as _np
    import concourse.bacc as _bacc
    from concourse import mybir as _mybir
    from concourse.bass_utils import run_bass_kernel_spmd as _run

    nc = _bacc.Bacc("TRN2", target_bir_lowering=False, num_devices=1)
    data = {name: _np.ascontiguousarray(inputs[name]) for name in _NAMES}
    given = [('x', data['x']), ('adj', data['adj']),
             ('adj_t', _np.ascontiguousarray(data['adj'].transpose(0, 2, 1)))]
    given += [(name, data[name]) for name in _NAMES[2:]]
    arrays, args = {}, []
    for name, a in given:
        arrays[f"in_{name}_dram"] = a
        args.append(nc.dram_tensor(f"in_{name}_dram", a.shape, _mybir.dt.from_np(a.dtype), kind="ExternalInput").ap())
    shape = data['x'].shape
    args.append(nc.dram_tensor("out_0_dram", shape, _mybir.dt.float32, kind="ExternalOutput").ap())
    graph_layers(nc, *args)
    r = _run(nc, [arrays], core_ids=[0])
    return r.results[0]["out_0_dram"]
```

```python
from contextlib import ExitStack

import concourse.bass as bass
from concourse import mybir

F32 = mybir.dt.float32
F32R = mybir.dt.float32r
ALU = mybir.AluOpType
ACT = mybir.ActivationFunctionType
AX_X = mybir.AxisListType.X

P = 128
SLOPE = 0.2
NORM_EPS = 1e-5
SUM_EPS = 1e-12


def graph_layers(nc, x, adj, adj_t, kern, bias, wv, bv, aw, ab, wk, bk, out):
    G, N, F = x.shape
    NB = N // P
    FB = F // P
    FS = NB // FB
    NE = F + 2
    S_J, S_I = F, F + 1
    assert NB == 4 and FB == 2 and G % 2 == 0

    x_rows = x.rearrange("g (b p) f -> (g b) p f", p=P)
    adj_rows = adj.rearrange("g (b p) m -> (g b) p m", p=P)
    adj_t_rows = adj_t.rearrange("g (b p) m -> (g b) p m", p=P)
    out_rows = out.rearrange("g (b p) f -> (g b) p f", p=P)

    def graph_of(rows, t):
        return rows[bass.ds(t, NB), :, :].rearrange("b p f -> p b f")

    with ExitStack() as ctx:
        def sb(name, shape, dt=F32):
            return ctx.enter_context(nc.sbuf_tensor(name, shape, dt))

        def sem(name):
            return ctx.enter_context(nc.semaphore(name))

        agg_ps = [ctx.enter_context(nc.psum_tensor(f"agg_ps{f}", [P, N], F32)) for f in range(FB)]
        ring = [ctx.enter_context(nc.psum_tensor(f"ring{i}", [P, 512], F32)) for i in range(NB)]
        turn_ps = [ctx.enter_context(nc.psum_tensor(f"turn_ps{f}", [P, N], F32)) for f in range(FB)]
        target_ps = turn_ps[0]

        def spare_ps(i):
            return agg_ps[i // 2][:, (i % 2) * F:(i % 2 + 1) * F]

        w2s_hi, w2s_lo = sb("w2s_hi", [P, FB, NE], F32R), sb("w2s_lo", [P, FB, NE], F32R)
        w1_hi, w1_lo = sb("w1_hi", [P, FB, F], F32R), sb("w1_lo", [P, FB, F], F32R)
        w0_hi, w0_lo = sb("w0_hi", [P, FB, F], F32R), sb("w0_lo", [P, FB, F], F32R)
        kern_hi, kern_lo = sb("kern_hi", [P, FB, F], F32R), sb("kern_lo", [P, FB, F], F32R)
        bias0 = sb("bias0", [P, F])
        bias1 = sb("bias1", [P, F])
        score_bias = sb("score_bias", [P, 1])
        ident = sb("ident", [P, P])
        ones4 = sb("ones4", [P, NB])
        minus_half = sb("minus_half", [P, NB])

        a_t = [sb(f"a_t{k}", [P, NB, N]) for k in range(2)]
        a_nat = sb("a_nat", [P, NB, N])
        xin = [sb(f"xin{k}", [P, NB, F]) for k in range(2)]
        ah_hi, ah_lo = sb("ah_hi", [P, NB, N], F32R), sb("ah_lo", [P, NB, N], F32R)
        diag = sb("diag", [P, NB, P])
        deg = sb("deg", [P, NB])
        deg1 = sb("deg1", [P, NB])
        dh = [sb(f"dh{k}", [P, NB]) for k in range(2)]
        xd_hi, xd_lo = sb("xd_hi", [P, NB, F], F32R), sb("xd_lo", [P, NB, F], F32R)
        y_hi, y_lo = sb("y_hi", [P, FB, N], F32R), sb("y_lo", [P, FB, N], F32R)
        h0 = sb("h0", [P, NB, F])
        r0 = sb("r0", [P, NB, F])
        x1 = [sb(f"x1_{k}", [P, NB, F]) for k in range(2)]
        x1t_hi, x1t_lo = sb("x1t_hi", [P, FB, N], F32R), sb("x1t_lo", [P, FB, N], F32R)
        score = sb("score", [P, NB, 2])
        sj = sb("sj", [P, NB])
        sj_slope = sb("sj_slope", [P, NB])
        u0 = sb("u0", [P, NB, F])
        u1 = sb("u1", [P, NB, F])
        v2_hi, v2_lo = sb("v2_hi", [P, NB, NE], F32R), sb("v2_lo", [P, NB, F], F32R)
        exp_a = sb("exp_a", [P, NB, N])
        exp_b = sb("exp_b", [P, NB, N])
        s_hi, s_lo = sb("s_hi", [P, NB, N], F32R), sb("s_lo", [P, NB, N], F32R)
        row_sum = sb("row_sum", [P, NB])
        row_inv = sb("row_inv", [P, NB])
        v1 = sb("v1", [P, NB, F])
        v1_hi, v1_lo = sb("v1_hi", [P, NB, F], F32R), sb("v1_lo", [P, NB, F], F32R)
        h1 = sb("h1", [P, NB, F])
        r1 = [sb(f"r1_{k}", [P, NB, F]) for k in range(2)]
        y_out = sb("y_out", [P, NB, F])
        stats = [sb(f"stats{k}", [P, NB, 6]) for k in range(2)]
        mean_var = [sb(f"mean_var{k}", [P, NB, 2]) for k in range(2)]
        var_eps = [sb(f"var_eps{k}", [P, NB]) for k in range(2)]
        rstd = [sb(f"rstd{k}", [P, NB]) for k in range(2)]
        shift = [sb(f"shift{k}", [P, NB]) for k in range(2)]
        pace = sb("pace", [P, 1])

        w2s_raw = exp_a[:, 0:2, :].rearrange("p b n -> p (b n)")[:, 0:FB * NE].rearrange("p (f n) -> p f n", f=FB)
        w1_raw = exp_b[:, 0, :].rearrange("p (f n) -> p f n", f=FB)
        w0_raw = exp_b[:, 1, :].rearrange("p (f n) -> p f n", f=FB)
        wv_raw = exp_a[:, 2, :].rearrange("p (f n) -> p f n", f=FB)
        kern_raw = exp_a[:, 3, :].rearrange("p (f n) -> p f n", f=FB)
        aw_rep = exp_b[:, 2, :]
        bv_rep = exp_b[:, 3, 0:F]
        dots = exp_b[:, 3, F:2 * F]
        bk_rep = h1[:, 0:3, :]
        ab_rep = sb("ab_rep", [P, 1])
        bv_dot = sb("bv_dot", [P, 2])

        ld_kernel = sem("ld_kernel")
        ld_w = sem("ld_w")
        ld_rep = sem("ld_rep")
        ld_at = [sem(f"ld_at{k}") for k in range(2)]
        ld_x = [sem(f"ld_x{k}") for k in range(2)]
        ld_nat = sem("ld_nat")
        out_free = sem("out_free")
        const_ready = sem("const_ready")
        set_dve = sem("set_dve")
        kernel_ready = sem("kernel_ready")
        weights_ready = sem("weights_ready")
        agg_done = sem("agg_done")
        kern_done = sem("kern_done")
        turn_done = sem("turn_done")
        u2_done = sem("u2_done")
        uw1_done = sem("uw1_done")
        uw0_done = sem("uw0_done")
        target_done = sem("target_done")
        sv2_done = sem("sv2_done")
        sv1_done = sem("sv1_done")
        ah_hi_done = sem("ah_hi_done")
        xd_hi_done = sem("xd_hi_done")
        y_hi_done = sem("y_hi_done")
        x1t_hi_done = sem("x1t_hi_done")
        v2_hi_done = sem("v2_hi_done")
        u1_done = sem("u1_done")
        u0_done = sem("u0_done")
        x1_done = sem("x1_done")
        exp_done = sem("exp_done")
        s_hi_done = sem("s_hi_done")
        v1_hi_done = sem("v1_hi_done")
        out_done = sem("out_done")
        last_out_done = sem("last_out_done")
        last_s_done = sem("last_s_done")
        last_relu_done = sem("last_relu_done")
        last_r1_done = sem("last_r1_done")
        xd_lo_done = sem("xd_lo_done")
        y_lo_done = sem("y_lo_done")
        h0_done = sem("h0_done")
        r0_done = sem("r0_done")
        stat0_done = sem("stat0_done")
        agr0_done = sem("agr0_done")
        eps0_done = sem("eps0_done")
        shift0_done = sem("shift0_done")
        x1t_lo_done = sem("x1t_lo_done")
        score_done = sem("score_done")
        sj_done = sem("sj_done")
        v2_lo_done = sem("v2_lo_done")
        max_done = sem("max_done")
        s_lo_done = sem("s_lo_done")
        sum_done = sem("sum_done")
        inv_done = sem("inv_done")
        v1_done = sem("v1_done")
        v1_lo_done = sem("v1_lo_done")
        h1_done = sem("h1_done")
        r1_done = sem("r1_done")
        stat1_done = sem("stat1_done")
        agr1_done = sem("agr1_done")
        eps1_done = sem("eps1_done")
        shift1_done = sem("shift1_done")
        deg_done = sem("deg_done")
        deg1_done = sem("deg1_done")
        dh_done = sem("dh_done")
        diag_done = sem("diag_done")
        s_done = sem("s_done")
        low_done = sem("low_done")
        ah_lo_done = sem("ah_lo_done")
        u0_bias_done = sem("u0_bias_done")
        rstd0_done = sem("rstd0_done")
        rstd1_done = sem("rstd1_done")

        def loaded(k, t):
            return t * 2 + (16 if k == 0 else 8)

        def loaded_at(k, t):
            return t * 8 + (64 if k == 0 else 32)

        def diagonal(tensor, width):
            full = tensor[:, 0, 0:P]
            return bass.AP(full.tensor, full.offset, [list(full.ap[0]), [width + P, NB], [1, P]])

        on_diagonal = ident[:, :].unsqueeze(1).to_broadcast([P, NB, P])

        block = ctx.enter_context(nc.Block())

        @block.sync
        def _(sp):
            def load_x(t, k):
                sp.dma_start(xin[k][:, :, :], graph_of(x_rows, t)).then_inc(ld_x[k], 16)

            def load_nat(t):
                sp.dma_start(a_nat[:, :, :], graph_of(adj_rows, t)).then_inc(ld_nat, 16)

            def load_at_block(t, k, j):
                sp.dma_start(a_t[k][:, j, :], adj_t_rows[bass.ds(t + j, 1), :, :].rearrange("b p f -> p (b f)"))\
                  .then_inc(ld_at[k], 16)

            def load_at(t, k):
                for j in range(NB):
                    load_at_block(t, k, j)

            def store(t):
                sp.wait_ge(out_done, t + 4)
                sp.dma_start(graph_of(out_rows, t), y_out[:, :, :]).then_inc(out_free, 16)

            def ahead(t, k):
                sp.wait_ge(x1_done, t + 4)
                load_x(t + 8, k)
                sp.wait_ge(deg_done, t + 8)
                load_nat(t + 8)
                for j in range(NB):
                    sp.wait_ge(s_done, t + j + 1)
                    load_at_block(t + 8, k, j)

            def load_weights(dst, w, landed):
                sp.dma_start(dst, w.rearrange("(f p) n -> p f n", p=P)).then_inc(landed, 16)

            load_at(0, 0)
            load_nat(0)
            load_x(0, 0)
            load_weights(kern_raw, kern, ld_kernel)
            load_weights(wv_raw, wv, ld_w)
            load_weights(w2s_raw[:, :, 0:F], wk[2], ld_w)
            load_weights(w1_raw, wk[1], ld_w)
            load_weights(w0_raw, wk[0], ld_w)
            sp.wait_ge(deg_done, 4)
            sp.wait_ge(ld_rep, 16 * 5)
            load_nat(4)
            load_x(4, 1)
            load_at(4, 1)
            ahead(0, 0)
            with sp.Fori(4, 4 * (G - 4) - 3, 8) as t0:
                for half in range(2):
                    t = t0 + 4 * half
                    ahead(t, 1 - half)
                    store(t - 4)
            ahead(4 * (G - 3), 1)
            for g in range(G - 4, G - 1):
                store(4 * g)
            for half in range(2):
                blocks = slice(2 * half, 2 * half + 2)
                sp.wait_ge(out_done, 4 * (G - 1) + half + 1)
                sp.wait_ge(last_out_done, half + 1)
                sp.dma_start(graph_of(out_rows, 4 * (G - 1))[:, blocks, :], y_out[:, blocks, :]).then_inc(out_free, 16)
            sp.wait_ge(out_free, 16 * (G + 2))

        @block.tensor
        def _(pe):
            def three_passes(dst, terms, start=True, stop=True):
                for n, (l_hi, l_lo, r_hi, r_lo) in enumerate(terms):
                    pe.matmul(dst[:, 0:r_hi.shape[-1]], l_hi, r_hi, start=(start and n == 0), stop=False)
                    pe.matmul(dst[:, 0:r_lo.shape[-1]], l_hi, r_lo, start=False, stop=False)
                    last = pe.matmul(dst[:, 0:r_hi.shape[-1]], l_lo, r_hi, start=False,
                                     stop=(stop and n == len(terms) - 1))
                return last

            def aggregate(t, between=None, early=False):
                pe.wait_ge(ah_lo_done, t + 4)
                pe.wait_ge(xd_lo_done, t + 4)
                for f in range(FB):
                    if not early:
                        pe.wait_ge(u0_done, t - 8 + FS * (f + 1))
                    cols = slice(f * P, (f + 1) * P)
                    terms = [(xd_hi[:, j, cols], xd_lo[:, j, cols], ah_hi[:, j, :], ah_lo[:, j, :])
                             for j in range(NB)]
                    if f == 0:
                        three_passes(agg_ps[f], terms[:1], stop=False)
                        if between:
                            between()
                        last = three_passes(agg_ps[f], terms[1:], start=False)
                    else:
                        last = three_passes(agg_ps[f], terms)
                    last.then_inc(agg_done, FS)

            def first_graph(features, product, done):
                for f in range(FB):
                    pe.wait_ge(features, FS * (f + 1))
                    for i in range(NB):
                        last = three_passes(ring[i], [product(f, i)], start=(f == 0), stop=(f == FB - 1))
                        if f == FB - 1:
                            last.then_inc(done, 1)

            def times_kernel(t):
                pe.wait_ge(y_lo_done, t + 4)
                for i in range(NB):
                    pe.wait_ge(u1_done, t - 4 + i + 1)
                    rows = slice(i * P, (i + 1) * P)
                    three_passes(ring[i], [(y_hi[:, f, rows], y_lo[:, f, rows], kern_hi[:, f, :], kern_lo[:, f, :])
                                           for f in range(FB)]).then_inc(kern_done, 1)

            def turn_x1(t, k, first=False):
                pe.wait_ge(x1_done, t + 4)
                for f in range(FB):
                    if not first:
                        pe.wait_ge(exp_done if f == 0 else x1t_lo_done, t)
                    for i in range(NB):
                        last = pe.transpose(turn_ps[f][:, i * P:(i + 1) * P], x1[k][:, i, f * P:(f + 1) * P],
                                            ident[:, :])
                    last.then_inc(turn_done, FS)

            def x1_rows(f, i):
                rows = slice(i * P, (i + 1) * P)
                return x1t_hi[:, f, rows], x1t_lo[:, f, rows]

            def times_w2(t):
                pe.wait_ge(x1t_lo_done, t + 4)
                for i in range(NB):
                    pe.wait_ge(h1_done, t - 4 + i + 1)
                    three_passes(ring[i], [(*x1_rows(f, i), w2s_hi[:, f, :], w2s_lo[:, f, :]) for f in range(FB)])\
                        .then_inc(u2_done, 1)

            def times_w1(t):
                for i in range(NB):
                    pe.wait_ge(v2_lo_done, t + i + 1)
                    three_passes(ring[i], [(*x1_rows(f, i), w1_hi[:, f, :], w1_lo[:, f, :]) for f in range(FB)])\
                        .then_inc(uw1_done, 1)

            def times_w0(t, last=False):
                pe.wait_ge(y_lo_done, t + 4 if last else t + 8)
                for i in range(NB):
                    three_passes(spare_ps(i), [(*x1_rows(f, i), w0_hi[:, f, :], w0_lo[:, f, :]) for f in range(FB)])\
                        .then_inc(uw0_done, 1)

            def spread_targets(t):
                pe.wait_ge(score_done, t + 4)
                for i in range(NB):
                    last = pe.transpose(target_ps[:, i * P:(i + 1) * P],
                                        score[:, i, 1:2].to_broadcast([P, P]), ident[:, :])
                last.then_inc(target_done, 4)

            def times_s_v2(t):
                for i in range(NB):
                    pe.wait_ge(h0_done, t + 4 + i + 1)
                    rows = slice(i * P, (i + 1) * P)
                    for j in range(NB):
                        if i == 0:
                            pe.wait_ge(s_lo_done, t + j + 1)
                        done = three_passes(ring[i], [(s_hi[:, j, rows], s_lo[:, j, rows], v2_hi[:, j, :],
                                                       v2_lo[:, j, :])], start=(j == 0), stop=(j == NB - 1))
                    done.then_inc(sv2_done, 1)

            def times_s_v2_by_source(t):
                for sources in ([0], [1], [2, 3]):
                    for i in range(NB):
                        if sources[0] == 0:
                            pe.wait_ge(u1_done, t + i + 1)
                        rows = slice(i * P, (i + 1) * P)
                        for j in sources:
                            if i == 0:
                                pe.wait_ge(s_lo_done, t + j + 1)
                            done = three_passes(ring[i], [(s_hi[:, j, rows], s_lo[:, j, rows], v2_hi[:, j, :],
                                                           v2_lo[:, j, :])], start=(j == 0), stop=(j == NB - 1))
                        if sources[-1] == NB - 1:
                            done.then_inc(sv2_done, 1)

            def times_s_v1(t, i, sources=range(NB)):
                pe.wait_ge(v1_lo_done, t + sources[-1] + 1)
                pe.wait_ge(v1_done, t + i + 1)
                rows = slice(i * P, (i + 1) * P)
                done = three_passes(ring[i], [(s_hi[:, j, rows], s_lo[:, j, rows], v1_hi[:, j, :], v1_lo[:, j, :])
                                              for j in sources], start=0 in sources, stop=NB - 1 in sources)
                if NB - 1 in sources:
                    done.then_inc(sv1_done, 1)

            def graph(t, k, first=False, last=False):
                if first:
                    pe.wait_ge(h0_done, 4)
                    first_graph(x1t_lo_done, lambda f, i: (*x1_rows(f, i), w2s_hi[:, f, :], w2s_lo[:, f, :]), u2_done)
                else:
                    times_w2(t)
                if last:
                    spread_targets(t)
                else:
                    aggregate(t + 4, between=lambda: spread_targets(t), early=first)
                times_w1(t)
                if not last:
                    times_kernel(t + 4)
                if last:
                    times_w0(t, last)
                    times_s_v2_by_source(t)
                    for j in range(2):
                        for i in range(NB):
                            times_s_v1(t, i, sources=[j])
                else:
                    times_s_v2(t)
                    times_w0(t)
                for i in range(NB):
                    times_s_v1(t, i, range(2 if last else 0, NB))
                    if i == 1 and not last:
                        turn_x1(t + 4, 1 - k)

            pe.wait_ge(const_ready, 4)
            aggregate(0, early=True)
            pe.wait_ge(kernel_ready, 1)
            first_graph(y_lo_done, lambda f, i: (y_hi[:, f, i * P:(i + 1) * P], y_lo[:, f, i * P:(i + 1) * P],
                                                 kern_hi[:, f, :], kern_lo[:, f, :]), kern_done)
            turn_x1(0, 0, first=True)
            pe.wait_ge(weights_ready, 1)
            graph(0, 0, first=True)
            with pe.Fori(4, 4 * (G - 2) - 3, 8) as t0:
                for half in range(2):
                    graph(t0 + 4 * half, 1 - half)
            graph(4 * (G - 1), 1, last=True)

        @block.scalar
        def _(act):
            def high_adj(t, k):
                act.wait_ge(ld_at[k], loaded_at(k, t))
                act.wait_ge(agg_done, t)
                act.activation(ah_hi[:, :, :], a_t[k][:, :, :], ACT.Copy).then_inc(ah_hi_done, 4)

            def row_sums(t, blocks=NB):
                act.wait_ge(ld_nat, t * 4 + 16)
                for i in range(blocks):
                    act.activation(a_nat[:, i, :], a_nat[:, i, :], ACT.Copy, accum_out=deg[:, i:i + 1])\
                       .then_inc(deg_done, 1)

            def high_xd(t, k, blocks=range(NB), first=False):
                if blocks[0] == 0:
                    act.wait_ge(ld_x[k], loaded(k, t))
                    act.wait_ge(dh_done, t + 4)
                    if not first:
                        act.wait_ge(agg_done, t)
                for i in blocks:
                    act.activation(xd_hi[:, i, :], xin[k][:, i, :], ACT.Copy, scale=dh[k][:, i:i + 1])\
                       .then_inc(xd_hi_done, 1)

            def high_y(t, f):
                act.wait_ge(agg_done, t + FS * (f + 1))
                act.activation(y_hi[:, f, :], agg_ps[f][:, :], ACT.Copy).then_inc(y_hi_done, FS)

            def high_x1t(t):
                for f in range(FB):
                    act.wait_ge(turn_done, t + FS * (f + 1))
                    act.activation(x1t_hi[:, f, :], turn_ps[f][:, :], ACT.Copy).then_inc(x1t_hi_done, FS)

            def high_v2(t):
                for i in range(NB):
                    act.wait_ge(score_done, t + i + 1)
                    act.activation(v2_hi[:, i, 0:F], ring[i][:, 0:F], ACT.Copy).then_inc(v2_hi_done, 1)

            def take_u1(t, i):
                act.wait_ge(uw1_done, t + i + 1)
                act.activation(u1[:, i, :], ring[i][:, 0:F], ACT.Copy).then_inc(u1_done, 1)

            def take_u0(t, i):
                act.wait_ge(uw0_done, t + 2 * (i // 2 + 1))
                act.activation(u0[:, i, :], spare_ps(i), ACT.Copy).then_inc(u0_done, 1)

            def norm_x1(t, k, i, ready=4):
                if i in (0, 2):
                    act.wait_ge(shift0_done, t + ready)
                act.activation(x1[k][:, i, :], r0[:, i, :], ACT.Identity, scale=rstd[0][:, i:i + 1],
                               bias=shift[0][:, i:i + 1]).then_inc(x1_done, 1)

            def exps(t, j):
                if j == 0:
                    act.wait_ge(target_done, t + 4)
                    act.wait_ge(sj_done, t + 4)
                act.activation(exp_a[:, j, :], target_ps[:, :], ACT.Exp, bias=sj[:, j:j + 1])
                act.activation(exp_b[:, j, :], target_ps[:, :], ACT.Exp, bias=sj_slope[:, j:j + 1], scale=SLOPE)\
                   .then_inc(exp_done, 1)

            def high_s(t, j, by_vector=False):
                if by_vector:
                    act.wait_ge(last_s_done, (j + 1) // 2)
                else:
                    act.wait_ge(s_done, t + j + 1)
                act.activation(s_hi[:, j, :], exp_b[:, j, :], ACT.Copy).then_inc(s_hi_done, 1)

            def high_v1(t, i, n):
                act.wait_ge(v1_done, t + i + n)
                act.activation(v1_hi[:, i:i + n, :], v1[:, i:i + n, :], ACT.Copy).then_inc(v1_hi_done, n)

            def norm_out(t, k, first_block, n=2):
                act.wait_ge(shift1_done, t + (first_block + 2 if n == 1 else 4))
                if first_block == 0:
                    act.wait_ge(out_free, t * 4 + 16)
                for i in range(first_block, first_block + n):
                    act.activation(y_out[:, i, :], r1[k][:, i, :], ACT.Identity, scale=rstd[1][:, i:i + 1],
                                   bias=shift[1][:, i:i + 1]).then_inc(out_done, 1)

            def graph(t, k, first=False, last=False, ahead=True):
                high_v2(t)
                for j in range(NB - 1):
                    exps(t, j)
                if last:
                    take_u1(t, 0)
                    high_s(t, 0)
                    for i in range(1, NB):
                        take_u1(t, i)
                    high_s(t, 1, by_vector=True)
                    exps(t, NB - 1)
                    high_s(t, 2)
                    high_s(t, 3, by_vector=True)
                else:
                    high_y(t + 4, 0)
                    exps(t, NB - 1)
                    high_y(t + 4, 1)
                    take_u1(t, 0)
                    high_s(t, 0)
                    high_s(t, 1)
                    take_u1(t, 1)
                    high_s(t, 2)
                    take_u1(t, 2)
                    high_s(t, 3)
                    take_u1(t, 3)
                if ahead:
                    row_sums(t + 8)
                    high_adj(t + 8, k)
                    high_xd(t + 8, k)
                if last:
                    for i in range(NB):
                        take_u0(t, i)
                    norm_out(t - 4, 1 - k, 0)
                    for i in range(NB):
                        high_v1(t, i, 1)
                    norm_out(t - 4, 1 - k, 2)
                    for i in range(2):
                        act.wait_ge(h1_done, t + i + 1)
                        act.activation(r1[k][:, i, :], h1[:, i, :], ACT.Relu).then_inc(last_relu_done, 1)
                else:
                    high_v1(t, 0, 2)
                    high_v1(t, 2, 1)
                    high_v1(t, 3, 1)
                    norm_x1(t + 4, 1 - k, 0)
                    take_u0(t, 0)
                    norm_x1(t + 4, 1 - k, 1)
                    take_u0(t, 1)
                    norm_x1(t + 4, 1 - k, 2)
                    take_u0(t, 2)
                    norm_x1(t + 4, 1 - k, 3)
                    take_u0(t, 3)
                    if not first:
                        norm_out(t - 4, 1 - k, 0)
                    high_x1t(t + 4)
                    if not first:
                        norm_out(t - 4, 1 - k, 2)

            row_sums(0, blocks=2)
            high_xd(0, 0, first=True)
            for dst, src in ((aw_rep, aw.rearrange("n one -> (n one)")), (bv_rep, bv), (bias0[:, :], bias),
                             (bk_rep, bk), (ab_rep[:, :], ab)):
                act.dma_start(dst, src.partition_broadcast(P)).then_inc(ld_rep, 16)
            high_y(0, 0)
            high_y(0, 1)
            row_sums(4)
            high_adj(4, 1)
            norm_x1(0, 0, 0, ready=2)
            high_xd(4, 1, range(2))
            norm_x1(0, 0, 2, ready=4)
            high_xd(4, 1, range(2, NB))
            high_x1t(0)
            graph(0, 0, first=True)
            with act.Fori(4, 4 * (G - 4) - 3, 8) as t0:
                for half in range(2):
                    graph(t0 + 4 * half, 1 - half)
            graph(4 * (G - 3), 1)
            graph(4 * (G - 2), 0, ahead=False)
            graph(4 * (G - 1), 1, last=True, ahead=False)
            norm_out(4 * (G - 1), 1, 0, n=1)
            norm_out(4 * (G - 1), 1, 2, n=1)

        @block.vector
        def _(dve):
            def low_xd(t, k, first_block):
                for i in range(first_block, first_block + 2):
                    dve.wait_ge(xd_hi_done, t + i + 1)
                    dve.scalar_tensor_tensor(xd_lo[:, i, :], xin[k][:, i, :], dh[k][:, i:i + 1],
                                             xd_hi[:, i, :].bitcast(F32), ALU.mult, ALU.subtract)\
                       .then_inc(xd_lo_done, 1)

            def low_y(t, f):
                dve.wait_ge(y_hi_done, t + FS * (f + 1))
                dve.tensor_tensor(y_lo[:, f, :], agg_ps[f][:, :], y_hi[:, f, :].bitcast(F32), ALU.subtract)\
                   .then_inc(y_lo_done, FS)

            def layer0_out(t, k, i):
                dve.wait_ge(kern_done, t + i + 1)
                dve.scalar_tensor_tensor(h0[:, i, :], ring[i][:, 0:F], dh[k][:, i:i + 1], bias0[:, :],
                                         ALU.mult, ALU.add).then_inc(h0_done, 1)

            def residual0(t, k, i):
                dve.wait_ge(h0_done, t + i + 1)
                dve.scalar_tensor_tensor(r0[:, i, :], h0[:, i, :], 0.0, xin[k][:, i, :],
                                         ALU.max, ALU.add).then_inc(r0_done, 1)

            def layer0_stats(t, i):
                dve.wait_ge(r0_done, t + i + 1)
                dve.bn_stats(stats[0][:, i, :], r0[:, i, :]).then_inc(stat0_done, 1)

            def moments(t, layer, stat_done, agr_done, i0=0, n=NB):
                dve.wait_ge(stat_done, t + i0 + n)
                dve.memset(pace[:, :], 0.0)
                for i in range(i0, i0 + n):
                    dve.bn_aggr(mean_var[layer][:, i, :], stats[layer][:, i, :]).then_inc(agr_done, 1)

            def add_eps(t, layer, agr_done, eps_done, i0=0, n=NB):
                dve.wait_ge(agr_done, t + i0 + n)
                dve.tensor_scalar(var_eps[layer][:, i0:i0 + n], mean_var[layer][:, i0:i0 + n, 1], NORM_EPS, None,
                                  ALU.add).then_inc(eps_done, n)

            def low_x1t(t):
                for f in range(FB):
                    dve.wait_ge(x1t_hi_done, t + FS * (f + 1))
                    dve.tensor_tensor(x1t_lo[:, f, :], turn_ps[f][:, :], x1t_hi[:, f, :].bitcast(F32), ALU.subtract)\
                       .then_inc(x1t_lo_done, FS)

            def take_v2(t):
                for s in range(NB + 1):
                    if s == NB:
                        source_scores(t)
                    if s < NB:
                        dve.wait_ge(u2_done, t + s + 1)
                        dve.tensor_copy(score[:, s, :], ring[s][:, S_J:S_I + 1]).then_inc(score_done, 1)
                    if s >= 1:
                        i = s - 1
                        dve.wait_ge(v2_hi_done, t + i + 1)
                        dve.tensor_tensor(v2_lo[:, i, :], ring[i][:, 0:F], v2_hi[:, i, 0:F].bitcast(F32),
                                          ALU.subtract).then_inc(v2_lo_done, 1)

            def source_scores(t):
                dve.wait_ge(score_done, t + 4)
                dve.tensor_scalar(sj[:, :], score[:, :, 0], score_bias[:, 0:1], None, ALU.add).then_inc(sj_done, 2)
                dve.tensor_scalar(sj_slope[:, :], score[:, :, 0], score_bias[:, 0:1], SLOPE, ALU.add, ALU.mult)\
                   .then_inc(sj_done, 2)

            def larger_exp(t, j):
                dve.wait_ge(exp_done, t + j + 1)
                dve.tensor_tensor(exp_a[:, j, :], exp_a[:, j, :], exp_b[:, j, :], ALU.max).then_inc(max_done, 1)

            def make_s(t, k, j):
                dve.wait_ge(ld_at[k], loaded_at(k, t))
                dve.wait_ge(max_done, t + j + 1)
                dve.tensor_tensor(exp_b[:, j, :], a_t[k][:, j, :], exp_a[:, j, :], ALU.mult)\
                   .then_inc(last_s_done, 1)

            def low_s(t, j):
                dve.wait_ge(s_hi_done, t + j + 1)
                dve.tensor_tensor(s_lo[:, j, :], exp_b[:, j, :], s_hi[:, j, :].bitcast(F32), ALU.subtract)\
                   .then_inc(s_lo_done, 1)

            def sum_rows(t, i):
                dve.wait_ge(sv2_done, t + i + 1)
                dve.tensor_scalar(row_sum[:, i:i + 1], ring[i][:, F:F + 1], SUM_EPS, None, ALU.add)\
                   .then_inc(sum_done, 1)

            def invert_rows(t, i):
                dve.wait_ge(sum_done, t + i + 1)
                dve.reciprocal(row_inv[:, i:i + 1], row_sum[:, i:i + 1]).then_inc(inv_done, 1)

            def make_v1(t, i):
                dve.wait_ge(inv_done, t + i + 1)
                dve.scalar_tensor_tensor(v1[:, i, :], ring[i][:, 0:F], row_inv[:, i:i + 1], u1[:, i, :],
                                         ALU.mult, ALU.add).then_inc(v1_done, 1)

            def low_v1(t, i, n):
                dve.wait_ge(v1_hi_done, t + i + n)
                dve.tensor_tensor(v1_lo[:, i:i + n, :], v1[:, i:i + n, :], v1_hi[:, i:i + n, :].bitcast(F32),
                                  ALU.subtract).then_inc(v1_lo_done, n)

            def make_h1(t, i):
                dve.wait_ge(sv1_done, t + i + 1)
                dve.wait_ge(u0_bias_done, t + i + 1)
                dve.scalar_tensor_tensor(h1[:, i, :], ring[i][:, 0:F], row_inv[:, i:i + 1], u0[:, i, :],
                                         ALU.mult, ALU.add).then_inc(h1_done, 1)

            def layer1_out(t, k, i, n=1, count=None):
                dve.wait_ge(h1_done, t + i + n)
                dve.scalar_tensor_tensor(r1[k][:, i:i + n, :], h1[:, i:i + n, :], 0.0, x1[k][:, i:i + n, :],
                                         ALU.max, ALU.add).then_inc(r1_done, count or n)

            def layer1_stats(t, k, i, by_pool=False):
                if by_pool:
                    dve.wait_ge(last_r1_done, i + 1)
                else:
                    dve.wait_ge(r1_done, t + i + 1)
                dve.bn_stats(stats[1][:, i, :], r1[k][:, i, :]).then_inc(stat1_done, 1)

            def shift_by(t, layer, rstd_done, shift_done, i0=0, n=NB):
                dve.wait_ge(rstd_done, t + i0 + n)
                dve.scalar_tensor_tensor(shift[layer][:, i0:i0 + n], mean_var[layer][:, i0:i0 + n, 0], -1.0,
                                         rstd[layer][:, i0:i0 + n], ALU.mult, ALU.mult).then_inc(shift_done, n)

            def norm_block(dst, src, layer, i):
                return dve.tensor_scalar(dst[:, i, :], src[:, i, :], rstd[layer][:, i:i + 1],
                                         shift[layer][:, i:i + 1], ALU.mult, ALU.add)

            def low_adj(t, k, j):
                dve.wait_ge(diag_done, t + 4)
                dve.tensor_tensor(ah_lo[:, j, :], a_t[k][:, j, :], ah_hi[:, j, :].bitcast(F32), ALU.subtract)\
                   .then_inc(low_done, 1)

            def graph(t, k, first=False, last=False, ahead=True):
                take_v2(t)
                if not first:
                    layer1_out(t - 4, 1 - k, 2, n=2)
                    layer1_stats(t - 4, 1 - k, 1)
                larger_exp(t, 0)
                if not first:
                    layer1_stats(t - 4, 1 - k, 2)
                    layer1_stats(t - 4, 1 - k, 3)
                larger_exp(t, 1)
                if last:
                    make_s(t, k, 1)
                if not first:
                    moments(t - 4, 1, stat1_done, agr1_done)
                larger_exp(t, 2)
                if last:
                    low_s(t, 0)
                    add_eps(t - 4, 1, agr1_done, eps1_done)
                    low_s(t, 1)
                    larger_exp(t, 3)
                    make_s(t, k, 3)
                    low_s(t, 2)
                    low_s(t, 3)
                else:
                    low_y(t + 4, 0)
                    larger_exp(t, 3)
                    low_y(t + 4, 1)
                    if not first:
                        add_eps(t - 4, 1, agr1_done, eps1_done)
                    low_s(t, 0)
                    low_s(t, 1)
                    low_s(t, 2)
                    layer0_out(t + 4, 1 - k, 0)
                    low_s(t, 3)
                if not last:
                    layer0_out(t + 4, 1 - k, 1)
                    residual0(t + 4, 1 - k, 0)
                    layer0_out(t + 4, 1 - k, 2)
                    residual0(t + 4, 1 - k, 1)
                    layer0_stats(t + 4, 0)
                    layer0_out(t + 4, 1 - k, 3)
                    residual0(t + 4, 1 - k, 2)
                    layer0_stats(t + 4, 1)
                    sum_rows(t, 0)
                    residual0(t + 4, 1 - k, 3)
                    invert_rows(t, 0)
                    layer0_stats(t + 4, 2)
                    make_v1(t, 0)
                    layer0_stats(t + 4, 3)
                    sum_rows(t, 1)
                    moments(t + 4, 0, stat0_done, agr0_done)
                    invert_rows(t, 1)
                    sum_rows(t, 2)
                    add_eps(t + 4, 0, agr0_done, eps0_done)
                    make_v1(t, 1)
                    invert_rows(t, 2)
                    sum_rows(t, 3)
                    make_v1(t, 2)
                    invert_rows(t, 3)
                    make_v1(t, 3)
                    shift_by(t + 4, 0, rstd0_done, shift0_done)
                    low_v1(t, 2, 1)
                    low_v1(t, 3, 1)
                else:
                    shift_by(t - 4, 1, rstd1_done, shift1_done)
                    sum_rows(t, 0)
                    invert_rows(t, 0)
                    for i in range(NB):
                        if i < NB - 1:
                            sum_rows(t, i + 1)
                        make_v1(t, i)
                        if i < NB - 1:
                            invert_rows(t, i + 1)
                        if i >= 1:
                            low_v1(t, i - 1, 1)
                    low_v1(t, NB - 1, 1)
                if not first and not last:
                    shift_by(t - 4, 1, rstd1_done, shift1_done)
                if ahead:
                    low_xd(t + 8, k, 0)
                    low_xd(t + 8, k, 2)
                if last:
                    for i in range(3):
                        make_h1(t, i)
                    layer1_stats(t, k, 0, by_pool=True)
                    make_h1(t, 3)
                    layer1_out(t, k, 2, count=3)
                    layer1_stats(t, k, 1, by_pool=True)
                    layer1_out(t, k, 3)
                    moments(t, 1, stat1_done, agr1_done, 0, 2)
                    layer1_stats(t, k, 2)
                    add_eps(t, 1, agr1_done, eps1_done, 0, 2)
                    layer1_stats(t, k, 3)
                    moments(t, 1, stat1_done, agr1_done, 2, 2)
                    add_eps(t, 1, agr1_done, eps1_done, 2, 2)
                else:
                    make_h1(t, 0)
                    if ahead:
                        low_adj(t + 8, k, NB - 1)
                    make_h1(t, 1)
                    layer1_out(t, k, 0)
                    layer1_stats(t, k, 0)
                    low_x1t(t + 4)
                    make_h1(t, 2)
                    layer1_out(t, k, 1)
                    make_h1(t, 3)

            dve.memset(v2_hi[:, :, F:F + 1].bitcast(F32), 1.0)
            dve.memset(v2_hi[:, :, F + 1:F + 2].bitcast(F32), 0.0)
            dve.wait_ge(ld_at[0], loaded_at(0, 0))
            dve.tensor_copy(ah_hi[:, :, :], a_t[0][:, :, :]).then_inc(ah_hi_done, 4)
            dve.wait_ge(const_ready, 4)
            dve.tensor_tensor(diag[:, :, :], diagonal(a_t[0], N), on_diagonal, ALU.add).then_inc(diag_done, 2)
            dve.wait_ge(ah_hi_done, 4)
            for half in (slice(0, 2), slice(2, 4)):
                dve.tensor_tensor(ah_lo[:, half, :], a_t[0][:, half, :], ah_hi[:, half, :].bitcast(F32),
                                  ALU.subtract).then_inc(low_done, 2)
                if half.start == 0:
                    dve.wait_ge(ld_nat, 16)
                    dve.tensor_reduce(deg[:, 2:4], a_nat[:, 2:4, :], AX_X, ALU.add).then_inc(deg_done, 2)
            dve.wait_ge(diag_done, 2)
            dve.wait_ge(low_done, 4)
            dve.tensor_copy(diagonal(ah_hi, N), diag[:, :, :]).then_inc(diag_done, 2)
            dve.wait_ge(diag_done, 4)
            dve.tensor_tensor(diagonal(ah_lo, N), diag[:, :, :], diagonal(ah_hi, N).bitcast(F32), ALU.subtract)\
               .then_inc(ah_lo_done, 4)
            low_xd(0, 0, 0)
            low_xd(0, 0, 2)
            dve.wait_ge(ld_kernel, 16)
            dve.tensor_copy(kern_hi[:, :, :], kern_raw).then_inc(set_dve, 1)
            dve.wait_ge(set_dve, 1)
            dve.tensor_tensor(kern_lo[:, :, :], kern_raw, kern_hi[:, :, :].bitcast(F32), ALU.subtract)\
               .then_inc(kernel_ready, 1)
            dve.wait_ge(ld_w, 16 * 4)
            dve.tensor_copy(w1_hi[:, :, :], w1_raw)
            dve.tensor_copy(w0_hi[:, :, :], w0_raw).then_inc(set_dve, 1)
            dve.wait_ge(set_dve, 2)
            dve.tensor_tensor(w1_lo[:, :, :], w1_raw, w1_hi[:, :, :].bitcast(F32), ALU.subtract)
            dve.tensor_tensor(w0_lo[:, :, :], w0_raw, w0_hi[:, :, :].bitcast(F32), ALU.subtract)
            dve.wait_ge(ld_rep, 16 * 5)
            done = 2
            for c in range(2):
                for f in range(FB):
                    dve.tensor_tensor_reduce(dots, wv_raw[:, f, :], aw_rep[:, c * F:(c + 1) * F], 1.0, 0.0, ALU.mult,
                                             ALU.add, w2s_raw[:, f, F + c:F + c + 1]).then_inc(set_dve, 1)
                    done += 1
                    dve.wait_ge(set_dve, done)
                dve.tensor_tensor_reduce(dots, bv_rep, aw_rep[:, c * F:(c + 1) * F], 1.0, 0.0, ALU.mult, ALU.add,
                                         bv_dot[:, c:c + 1]).then_inc(set_dve, 1)
                done += 1
                dve.wait_ge(set_dve, done)
            low_y(0, 0)
            dve.tensor_copy(w2s_hi[:, :, :], w2s_raw)
            dve.scalar_tensor_tensor(score_bias[:, :], bv_dot[:, 0:1], ab_rep[:, :], bv_dot[:, 1:2],
                                     ALU.add, ALU.add)
            dve.tensor_tensor(bias1[:, :], bk_rep[:, 0, :], bk_rep[:, 1, :], ALU.add).then_inc(set_dve, 1)
            done += 1
            low_y(0, 1)
            for s in range(NB + 2):
                if s < NB:
                    layer0_out(0, 0, s)
                if s >= 2:
                    layer0_stats(0, s - 2)
                if 1 <= s <= NB:
                    residual0(0, 0, s - 1)
                if s in (3, 5):
                    moments(0, 0, stat0_done, agr0_done, s - 3, 2)
                    add_eps(0, 0, agr0_done, eps0_done, s - 3, 2)
            for i in (0, 2):
                shift_by(0, 0, rstd0_done, shift0_done, i, 2)
                dve.wait_ge(shift0_done, i + 2)
                norm_block(x1[0], r0, 0, i + 1).then_inc(x1_done, 1)
                if i == 0:
                    dve.wait_ge(set_dve, done)
                    dve.tensor_tensor(w2s_lo[:, :, :], w2s_raw, w2s_hi[:, :, :].bitcast(F32), ALU.subtract)
                    dve.tensor_tensor(bias1[:, :], bias1[:, :], bk_rep[:, 2, :], ALU.add).then_inc(weights_ready, 1)
            low_adj(4, 1, NB - 1)
            low_x1t(0)
            low_xd(4, 1, 0)
            low_xd(4, 1, 2)
            dve.wait_ge(weights_ready, 1)
            graph(0, 0, first=True)
            with dve.Fori(4, 4 * (G - 4) - 3, 8) as t0:
                for half in range(2):
                    graph(t0 + 4 * half, 1 - half)
            graph(4 * (G - 3), 1)
            graph(4 * (G - 2), 0, ahead=False)
            graph(4 * (G - 1), 1, last=True, ahead=False)
            for i in (0, 2):
                shift_by(4 * (G - 1), 1, rstd1_done, shift1_done, i, 2)
                dve.wait_ge(out_free, 4 * 4 * (G - 1) + 16)
                dve.wait_ge(shift1_done, 4 * (G - 1) + i + 2)
                norm_block(y_out, r1[1], 1, i + 1).then_inc(last_out_done, 1)

        @block.gpsimd
        def _(pool):
            def make_s(t, k, j, last=False):
                if j == 0:
                    pool.wait_ge(ld_at[k], loaded_at(k, t))
                pool.wait_ge(max_done, t + j + 1)
                pool.tensor_tensor(exp_b[:, j, :], a_t[k][:, j, :], exp_a[:, j, :], ALU.mult)\
                    .then_inc(s_done, 2 if last else 1)

            def degrees(t, k):
                pool.wait_ge(deg_done, t + 4)
                pool.tensor_tensor(deg1[:, :], deg[:, :], ones4[:, :], ALU.add).then_inc(deg1_done, 4)
                pool.wait_ge(deg1_done, t + 4)
                pool.tensor_tensor(dh[k][:, :], deg1[:, :], minus_half[:, :], ALU.pow).then_inc(dh_done, 4)

            def add_identity(t, k):
                pool.wait_ge(ld_at[k], loaded_at(k, t))
                pool.wait_ge(ah_lo_done, t)
                pool.tensor_tensor(diag[:, :, :], diagonal(a_t[k], N), on_diagonal, ALU.add).then_inc(diag_done, 2)

            def high_diagonal(t, k):
                pool.wait_ge(ah_hi_done, t + 4)
                pool.tensor_tensor(diagonal(ah_hi, N), diagonal(a_t[k], N), on_diagonal, ALU.add)\
                    .then_inc(diag_done, 2)

            def low_adj(t, k, j):
                if j == 0:
                    pool.wait_ge(diag_done, t + 4)
                pool.tensor_tensor(ah_lo[:, j, :], a_t[k][:, j, :], ah_hi[:, j, :].bitcast(F32), ALU.subtract)\
                    .then_inc(low_done, 1)

            def low_diagonal(t):
                pool.wait_ge(low_done, t + 4)
                pool.tensor_tensor(diagonal(ah_lo, N), diag[:, :, :], diagonal(ah_hi, N).bitcast(F32),
                                   ALU.subtract).then_inc(ah_lo_done, 4)

            def add_bias(t, i):
                pool.wait_ge(u0_done, t + i + 1)
                pool.tensor_tensor(u0[:, i, :], u0[:, i, :], bias1[:, :], ALU.add).then_inc(u0_bias_done, 1)

            def root(t, layer, eps_done, rstd_done, i=0, n=NB):
                pool.wait_ge(eps_done, t + i + n)
                pool.tensor_tensor(rstd[layer][:, i:i + n], var_eps[layer][:, i:i + n], minus_half[:, 0:n], ALU.pow)\
                    .then_inc(rstd_done, n)

            def low_v1(t, i, n):
                pool.wait_ge(v1_hi_done, t + i + n)
                pool.tensor_tensor(v1_lo[:, i:i + n, :], v1[:, i:i + n, :], v1_hi[:, i:i + n, :].bitcast(F32),
                                   ALU.subtract).then_inc(v1_lo_done, n)

            def graph(t, k, first=False, last=False, ahead=True):
                for j in range(0, NB, 2 if last else 1):
                    make_s(t, k, j, last)
                if not first:
                    root(t - 4, 1, eps1_done, rstd1_done)
                if ahead:
                    degrees(t + 8, k)
                    add_identity(t + 8, k)
                if not last:
                    root(t + 4, 0, eps0_done, rstd0_done)
                    low_v1(t, 0, 2)
                if ahead:
                    high_diagonal(t + 8, k)
                for i in range(NB):
                    add_bias(t, i)
                    if ahead and i < NB - 1:
                        low_adj(t + 8, k, i)
                if ahead:
                    low_diagonal(t + 8)

            pool.memset(ident[:, :], 0.0).then_inc(const_ready, 1)
            pool.memset(ones4[:, :], 1.0).then_inc(const_ready, 1)
            pool.memset(minus_half[:, :], -0.5).then_inc(const_ready, 1)
            pool.wait_ge(const_ready, 3)
            pool.affine_select(out=ident[:, :], in_=ident[:, :], compare_op=ALU.not_equal, fill=1.0, base=0,
                               pattern=[[-1, P]], channel_multiplier=1).then_inc(const_ready, 1)
            pool.wait_ge(const_ready, 4)
            pool.memset(y_out[:, 0, 0:1], 0.0).then_inc(out_free, 16)
            degrees(0, 0)
            degrees(4, 1)
            add_identity(4, 1)
            root(0, 0, eps0_done, rstd0_done, 0, 2)
            high_diagonal(4, 1)
            root(0, 0, eps0_done, rstd0_done, 2, 2)
            low_adj(4, 1, 0)
            low_adj(4, 1, 1)
            low_adj(4, 1, 2)
            low_diagonal(4)
            pool.wait_ge(weights_ready, 1)
            graph(0, 0, first=True)
            with pool.Fori(4, 4 * (G - 4) - 3, 8) as t0:
                for half in range(2):
                    graph(t0 + 4 * half, 1 - half)
            graph(4 * (G - 3), 1)
            graph(4 * (G - 2), 0, ahead=False)
            graph(4 * (G - 1), 1, last=True, ahead=False)
            for i in range(2):
                pool.wait_ge(last_relu_done, i + 1)
                pool.tensor_tensor(r1[1][:, i, :], r1[1][:, i, :], x1[1][:, i, :], ALU.add).then_inc(last_r1_done, 1)
            pool.wait_ge(out_done, 4 * (G - 1))
            root(4 * (G - 1), 1, eps1_done, rstd1_done, 0, 2)
            root(4 * (G - 1), 1, eps1_done, rstd1_done, 2, 2)


_NAMES = ['x', 'adj', 'L0_gnn_kernel', 'L0_gnn_bias', 'L1_gnn_Wv', 'L1_gnn_bv', 'L1_gnn_aw', 'L1_gnn_ab',
          'L1_gnn_Wk', 'L1_gnn_bk']


def kernel(**inputs):
    import numpy as _np
    import concourse.bacc as _bacc
    from concourse import mybir as _mybir
    from concourse.bass_utils import run_bass_kernel_spmd as _run

    nc = _bacc.Bacc("TRN2", target_bir_lowering=False, num_devices=1)
    data = {name: _np.ascontiguousarray(inputs[name]) for name in _NAMES}
    given = [('x', data['x']), ('adj', data['adj']),
             ('adj_t', _np.ascontiguousarray(data['adj'].transpose(0, 2, 1)))]
    given += [(name, data[name]) for name in _NAMES[2:]]
    arrays, args = {}, []
    for name, a in given:
        arrays[f"in_{name}_dram"] = a
        args.append(nc.dram_tensor(f"in_{name}_dram", a.shape, _mybir.dt.from_np(a.dtype), kind="ExternalInput").ap())
    shape = data['x'].shape
    args.append(nc.dram_tensor("out_0_dram", shape, _mybir.dt.float32, kind="ExternalOutput").ap())
    graph_layers(nc, *args)
    r = _run(nc, [arrays], core_ids=[0])
    return r.results[0]["out_0_dram"]
```
